# Optimizing a Trainium2 kernel written in Bass

```python
import numpy as np
import jax
import jax.numpy as jnp

def _softmax(x, axis=-1):
    return jax.nn.softmax(x, axis=axis)

def _gelu(x):
    return jax.nn.gelu(x, approximate=True)

def _silu(x):
    return jax.nn.silu(x)

def _sigmoid(x):
    return jax.nn.sigmoid(x)

def _layernorm(x, axis=-1, eps=1e-05):
    m = jnp.mean(x, axis=axis, keepdims=True)
    v = jnp.var(x, axis=axis, keepdims=True)
    return (x - m) / jnp.sqrt(v + eps)

def _scatter_add(tgt, idx, src, axis=0):
    return tgt.at[idx].add(src)

def _segment_sum(src, seg, n):
    return jax.ops.segment_sum(src, seg, n)
kernel_name = 'mk_adaln_ffn_d1_seqx_r8_032b1b'

def setup_inputs(seed: int=0):
    np.random.seed(seed)
    _w = jnp.asarray

    def _rec_inputs():
        import jax
        import jax.numpy as jnp
        _rk = jax.random.key(seed)
        x = -8.015e-05 + 0.9999 * jax.random.normal(jax.random.fold_in(_rk, 1), (64, 32, 256), jnp.float32)
        _lenS = 32 - jax.random.randint(jax.random.fold_in(_rk, 7), (64,), 0, max(1, 32 // 4) + 1, jnp.int32)
        _lenS2 = 32 - jax.random.randint(jax.random.fold_in(_rk, 8), (64,), 0, max(1, 32 // 4) + 1, jnp.int32)
        cond_1024 = 0.00191187 + 0.999416 * jax.random.normal(jax.random.fold_in(_rk, 11), (64, 128), jnp.float32)
        return (x, cond_1024)
    x, cond_1024 = _rec_inputs()

    def _L0_cond_setup():
        import jax, jax.numpy as jnp
        import numpy as np
        B, N, V_DIM, Q_DIM = (32, 100, 256, 128)
        key = jax.random.key(seed)
        k1, k2, k3, k4 = jax.random.split(key, 4)
        v = jax.random.normal(k1, (B, N, V_DIM), dtype=jnp.float32)
        q = jax.random.normal(k2, (B, Q_DIM), dtype=jnp.float32)
        W3 = jax.random.normal(k3, (Q_DIM, V_DIM), dtype=jnp.float32) * (1.0 / np.sqrt(Q_DIM))
        b3 = jnp.zeros((V_DIM,), dtype=jnp.float32)
        W2 = jax.random.normal(k4, (V_DIM, V_DIM), dtype=jnp.float32) * (1.0 / np.sqrt(V_DIM))
        b2 = jnp.zeros((V_DIM,), dtype=jnp.float32)
        return {'v': v, 'q': q, 'W3': W3, 'b3': b3, 'W2': W2, 'b2': b2}
    _L0_cond_all = _L0_cond_setup()
    _L0_cond_in = {k: v for k, v in _L0_cond_all.items() if k in ('W3', 'b3', 'W2', 'b2')}
    del _L0_cond_all

    def _L0_ffn_setup():
        import jax, jax.numpy as jnp
        import numpy as np
        from jax import lax
        H = 256
        I = 176
        E = 16
        TOP_K = 6
        IS = 2 * I

        def _swiglu(x, w13_, w2_):
            gu = x @ w13_.T
            g, u = jnp.split(gu, 2, axis=-1)
            return jax.nn.silu(g) * u @ w2_.T
        key = jax.random.key(seed)
        ks = jax.random.split(key, 6)
        return {'hidden_states': jax.random.normal(ks[0], (1, 256, H), jnp.float32), 'gate_w': jax.random.normal(ks[1], (E, H), jnp.float32) * 0.02, 'w13': jax.random.normal(ks[2], (E, 2 * I, H), jnp.float32) * 0.02, 'w2': jax.random.normal(ks[3], (E, H, I), jnp.float32) * 0.02, 'sw13': jax.random.normal(ks[4], (2 * IS, H), jnp.float32) * 0.02, 'sw2': jax.random.normal(ks[5], (H, IS), jnp.float32) * 0.02}
    _L0_ffn_all = _L0_ffn_setup()
    _L0_ffn_in = {k: v for k, v in _L0_ffn_all.items() if k in ('gate_w', 'w13', 'w2', 'sw13', 'sw2')}
    del _L0_ffn_all
    return {'x': x, 'cond_1024': cond_1024, 'L0_cond_W3': _L0_cond_in['W3'], 'L0_cond_b3': _L0_cond_in['b3'], 'L0_cond_W2': _L0_cond_in['W2'], 'L0_cond_b2': _L0_cond_in['b2'], 'L0_ffn_gate_w': _L0_ffn_in['gate_w'], 'L0_ffn_w13': _L0_ffn_in['w13'], 'L0_ffn_w2': _L0_ffn_in['w2'], 'L0_ffn_sw13': _L0_ffn_in['sw13'], 'L0_ffn_sw2': _L0_ffn_in['sw2']}

def reference(x, cond_1024, L0_cond_W3, L0_cond_b3, L0_cond_W2, L0_cond_b2, L0_ffn_gate_w, L0_ffn_w13, L0_ffn_w2, L0_ffn_sw13, L0_ffn_sw2):
    import jax
    import jax.numpy as jnp

    def _L0_cond_ref(v, q, W3, b3, W2, b2):
        import jax, jax.numpy as jnp
        import numpy as np
        B, N, V_DIM, Q_DIM = (32, 100, 256, 128)
        q_emb = jax.nn.relu(q @ W3 + b3)
        n = v.shape[1]
        v_sum = jnp.sum(v, axis=1, keepdims=True)
        x = (n * v + v_sum) * q_emb[:, None, :]
        return jax.nn.relu(x @ W2 + b2)

    def _L0_ffn_ref(hidden_states, gate_w, w13, w2, sw13, sw2):
        import jax, jax.numpy as jnp
        import numpy as np
        from jax import lax
        H = 256
        I = 176
        E = 16
        TOP_K = 6
        IS = 2 * I

        def _swiglu(x, w13_, w2_):
            gu = x @ w13_.T
            g, u = jnp.split(gu, 2, axis=-1)
            return jax.nn.silu(g) * u @ w2_.T
        B, S, Hd = hidden_states.shape
        x = hidden_states.reshape(-1, Hd)
        T = x.shape[0]
        scores = jax.nn.softmax(x @ gate_w.T, axis=-1)
        topk_w, topk_ids = lax.top_k(scores, TOP_K)
        topk_w = topk_w / (topk_w.sum(-1, keepdims=True) + 1e-20)
        combine = jnp.einsum('tk,tke->te', topk_w, jax.nn.one_hot(topk_ids, E, dtype=topk_w.dtype))

        def body(acc, ew):
            w13_e, w2_e, c_e = ew
            y = _swiglu(x, w13_e, w2_e)
            return (acc + c_e[:, None] * y, None)
        out, _ = lax.scan(body, jnp.zeros_like(x), (w13, w2, combine.T))
        out = out + _swiglu(x, sw13, sw2)
        return out.reshape(B, S, Hd)
    x = x + _L0_ffn_ref(_L0_cond_ref(x, cond_1024, L0_cond_W3, L0_cond_b3, L0_cond_W2, L0_cond_b2), L0_ffn_gate_w, L0_ffn_w13, L0_ffn_w2, L0_ffn_sw13, L0_ffn_sw2)
    return x

_drawn_inputs = setup_inputs


def setup_inputs(seed=0):
    import zlib

    import numpy as np

    out = dict(_drawn_inputs(seed))
    spreads = {'L0_cond_b3': (0.0, 0.1), 'L0_cond_b2': (0.0, 0.8)}
    factors = {}
    for name, (base, spread) in spreads.items():
        noise = np.random.default_rng([zlib.crc32(name.encode()), seed]).standard_normal(out[name].shape)
        drawn = base * np.exp(spread * noise) if base else spread * noise
        out[name] = jnp.asarray(drawn.astype(out[name].dtype))
    for name, factor in factors.items():
        out[name] = (out[name] * factor).astype(out[name].dtype)
    return out
```

```python
from contextlib import ExitStack

import concourse.bass as bass
from concourse import mybir
from concourse.alu_op_type import AluOpType as ALU

P = 128
F32 = mybir.dt.float32
F32R = mybir.dt.float32r
BF16 = mybir.dt.bfloat16
ACT = mybir.ActivationFunctionType
AX = mybir.AxisListType


def adaln_moe_ffn(nc, xT, qT, w3, b3, w2c, b2, gateT, w13T, w2T, sel, ident, outT, top_k):
    KC, T = xT.shape[1], xT.shape[2]
    B = qT.shape[1]
    N = T // B
    E = gateT.shape[2]
    J = w13T.shape[0]
    GT = 512
    NG = T // GT
    BG = GT // N
    TT = T // P
    TG = GT // P
    CE = 3 * E + 1

    with ExitStack() as ctx:
        def sb(name, shape, dt=F32):
            return ctx.enter_context(nc.sbuf_tensor(name, shape, dt))

        def sem(name):
            return ctx.enter_context(nc.semaphore(name))

        w13_hi = sb("w13_hi", [P, J, KC, 2 * P], F32R)
        w13_lo = sb("w13_lo", [P, J, KC, 2 * P], F32R)
        w2_hi = sb("w2_hi", [P, J, KC * P], F32R)
        w2_lo = sb("w2_lo", [P, J, KC * P], F32R)
        w13_raw = sb("w13_raw", [P, 2, KC, 2 * P])
        w2_raw = sb("w2_raw", [P, 2, KC * P])
        x_g = sb("x_g", [P, KC, GT])
        z_g = sb("z_g", [P, KC, GT])
        hid = sb("hid", [P, KC, GT])
        hid_hi = sb("hid_hi", [P, KC, GT], F32R)
        hid_lo = sb("hid_lo", [P, KC, GT], F32R)
        vsum = sb("vsum", [P, KC, BG])
        q_sb = sb("q_sb", [P, B])
        w3_sb = sb("w3_sb", [P, KC * P])
        b3_sb = sb("b3_sb", [P, KC])
        w2c_sb = sb("w2c_sb", [P, KC, KC * P])
        b2_sb = sb("b2_sb", [P, KC])
        gate_sb = sb("gate_sb", [P, KC, E])
        sel_sb = sb("sel_sb", [CE, J * P], BF16)
        ident_sb = sb("ident_sb", [P, P])
        qemb = sb("qemb", [P, KC, B])
        act = sb("act", [P, 2, GT])
        act_hi = sb("act_hi", [P, 2, GT], F32R)
        act_lo = sb("act_lo", [P, 2, GT], F32R)
        y_sb = sb("y_sb", [P, KC, GT])
        rmax = sb("rmax", [P, TG])
        shifted = sb("shifted", [P, TG, E])
        expd = sb("expd", [P, TG, E])
        esum = sb("esum", [P, TG])
        erec = sb("erec", [P, TG])
        score = sb("score", [P, TG, E])
        top = sb("top", [P, TG, 8])
        left = sb("left", [P, TG, E])
        chosen = sb("chosen", [P, TG, E])
        wsum = sb("wsum", [P, TG])
        comb = sb("comb", [P, TG, E])
        part_b = sb("part_b", [P, TG, E], BF16)
        rest = sb("rest", [P, 2, TG, E])
        apart = sb("apart", [P, 1])
        parts = sb("parts", [P, TG, CE])
        combT = sb("combT", [CE, GT], BF16)

        ps = [ctx.enter_context(nc.psum_tensor(f"bank{i}", [P, GT], F32)) for i in range(8)]
        ps_g, ps_u, ps_c, ps_y = ps[0:2], ps[2:4], ps[4:6], ps[6:8]

        s_const = sem("const_loaded")
        s_w13in = [sem(f"w13_loaded{i}") for i in range(2)]
        s_w2in = [sem(f"w2_loaded{i}") for i in range(2)]
        s_wsplit = sem("weights_split")
        s_whi = sem("weights_hi_done")
        s_xin = sem("x_loaded")
        s_qps = sem("qemb_in_psum")
        s_qemb = sem("qemb_ready")
        s_vsum = sem("vsum_ready")
        s_zx = sem("z_scaled")
        s_z = sem("z_ready")
        s_condps = sem("cond_in_psum")
        s_hid = sem("hid_ready")
        s_hhi = sem("hid_hi_ready")
        s_hlo = sem("hid_lo_ready")
        s_logit = sem("logits_in_psum")
        s_r = sem("routing_step")
        s_exp = sem("exp_ready")
        s_ones = sem("ones_row_set")
        s_partsT = sem("parts_transposed")
        s_combT = sem("combT_ready")
        s_gu = sem("gate_up_in_psum")
        s_c = sem("weight_in_psum")
        s_silu = sem("silu_ready")
        s_su = sem("silu_times_up")
        s_act = sem("act_ready")
        s_ahi = sem("act_hi_ready")
        s_alo = sem("act_lo_ready")
        s_down = sem("down_done")
        s_y = sem("y_added")
        s_out = sem("out_stored")

        block = ctx.enter_context(nc.Block())

        @block.sync
        def _(sp):
            for dst, src in ((q_sb, qT), (w3_sb, w3), (b3_sb, b3)):
                sp.dma_start(dst[:, :], src).then_inc(s_const, 16)
            sp.dma_start(w2c_sb[:, :, :], w2c).then_inc(s_const, 16)
            sp.dma_start(b2_sb[:, :], b2).then_inc(s_const, 16)
            sp.dma_start(x_g[:, :, :], xT[:, :, 0:GT]).then_inc(s_xin, 16)
            sp.dma_start(gate_sb[:, :, :], gateT).then_inc(s_const, 16)
            sp.dma_start(ident_sb[:, :], ident).then_inc(s_const, 16)
            sp.dma_start(sel_sb[:, :], sel).then_inc(s_const, 16)
            for j in range(J):
                if j >= 2:
                    sp.wait_ge(s_wsplit, 2 * (j - 1))
                sp.dma_start(w13_raw[:, j % 2], w13T[j]).then_inc(s_w13in[j % 2], 16)
                sp.dma_start(w2_raw[:, j % 2], w2T[j]).then_inc(s_w2in[j % 2], 16)
            with sp.Fori(0, NG - 1) as g:
                sp.wait_ge(s_y, g * KC + KC)
                sp.dma_start(outT[:, :, bass.ds(g * GT, GT)], y_sb[:, :, :]).then_inc(s_out, 16)
                sp.dma_start(x_g[:, :, :], xT[:, :, bass.ds(g * GT + GT, GT)]).then_inc(s_xin, 16)
            sp.wait_ge(s_y, NG * KC)
            sp.dma_start(outT[:, :, (NG - 1) * GT:], y_sb[:, :, :]).then_inc(s_out, 16)
            sp.wait_ge(s_out, 16 * NG)

        @block.gpsimd
        def _(pool):
            for j in range(J):
                pool.wait_ge(s_whi, 2 * j + 1)
                nc.gpsimd.tensor_sub(w13_lo[:, j], w13_raw[:, j % 2], w13_hi[:, j].bitcast(F32)).then_inc(s_wsplit, 1)
                pool.wait_ge(s_whi, 2 * j + 2)
                nc.gpsimd.tensor_sub(w2_lo[:, j], w2_raw[:, j % 2], w2_hi[:, j].bitcast(F32)).then_inc(s_wsplit, 1)

        CHAIN = 21

        @block.scalar
        def _(act_e):
            act_e.wait_ge(s_qps, 1)
            for k in range(KC):
                last = nc.scalar.activation(qemb[:, k], ps_c[0][:, k * B:(k + 1) * B], ACT.Relu, bias=b3_sb[:, k:k + 1])
            last.then_inc(s_qemb, 1)

            def split_weights(j):
                act_e.wait_ge(s_w13in[j % 2], 16 * (j // 2 + 1))
                nc.scalar.activation(w13_hi[:, j], w13_raw[:, j % 2], ACT.Copy).then_inc(s_whi, 1)
                act_e.wait_ge(s_w2in[j % 2], 16 * (j // 2 + 1))
                nc.scalar.activation(w2_hi[:, j], w2_raw[:, j % 2], ACT.Copy).then_inc(s_whi, 1)

            def group(g, first):
                act_e.wait_ge(s_condps, g + 1)
                for m in range(KC):
                    nc.scalar.activation(hid[:, m], ps_g[m][:, :], ACT.Relu, bias=b2_sb[:, m:m + 1]).then_inc(s_hid, 1)
                act_e.wait_ge(s_hid, g * KC + KC)
                nc.scalar.activation(hid_hi[:, :, :], hid[:, :, :], ACT.Copy).then_inc(s_hhi, 1)
                if first:
                    split_weights(0)
                    split_weights(1)
                act_e.wait_ge(s_r, g * CHAIN + 2)
                nc.scalar.activation(expd[:, :, :], shifted[:, :, :], ACT.Exp).then_inc(s_exp, 1)
                for j in range(J):
                    if first and j + 2 < J:
                        split_weights(j + 2)
                    act_e.wait_ge(s_gu, g * J + (j + 1))
                    if j >= 2:
                        act_e.wait_ge(s_alo, g * J + (j - 1))
                    nc.scalar.activation(act[:, j % 2], ps_g[j % 2][:, :], ACT.Silu).then_inc(s_silu, 1)
                    act_e.wait_ge(s_act, g * J + (j + 1))
                    if j >= 2:
                        act_e.wait_ge(s_down, g * J + (j - 1))
                    nc.scalar.activation(act_hi[:, j % 2], act[:, j % 2], ACT.Copy).then_inc(s_ahi, 1)

            group(0, True)
            with act_e.Fori(1, NG) as g:
                group(g, False)

        @block.vector
        def _(dve):
            nc.vector.memset(parts[:, :, 3 * E:], 1.0).then_inc(s_ones, 1)
            with dve.Fori(0, NG) as g:
                dve.wait_ge(s_xin, g * 16 + 16)
                x4 = x_g[:, :, :].rearrange("p k (b n) -> p k b n", n=N)
                z4 = z_g[:, :, :].rearrange("p k (b n) -> p k b n", n=N)
                nc.vector.tensor_reduce(vsum[:, :, :], x4, AX.X, ALU.add).then_inc(s_vsum, 1)
                dve.wait_ge(s_vsum, g + 1)
                for k in range(KC):
                    nc.vector.scalar_tensor_tensor(
                        z4[:, k], x4[:, k], float(N), vsum[:, k, :].unsqueeze(2).to_broadcast([P, BG, N]),
                        ALU.mult, ALU.add).then_inc(s_zx, 1)
                dve.wait_ge(s_zx, g * KC + KC)
                dve.wait_ge(s_qemb, 1)
                for k in range(KC):
                    nc.vector.tensor_tensor(
                        z4[:, k], z4[:, k],
                        qemb[:, k, bass.ds(g * BG, BG)].unsqueeze(2).to_broadcast([P, BG, N]),
                        ALU.mult).then_inc(s_z, 1)
                dve.wait_ge(s_hhi, g + 1)
                nc.vector.tensor_tensor(hid_lo[:, :, :], hid[:, :, :], hid_hi[:, :, :].bitcast(F32),
                                        ALU.subtract).then_inc(s_hlo, 1)
                step = [0]

                def chain(ins):
                    step[0] += 1
                    ins.then_inc(s_r, 1)
                    dve.wait_ge(s_r, g * CHAIN + step[0])

                def bc(a):
                    return a.unsqueeze(2).to_broadcast([P, TG, E])

                lg = ps_c[1][:, 0:TG * E].rearrange("p (t e) -> p t e", e=E)
                dve.wait_ge(s_logit, g + 1)
                chain(nc.vector.tensor_reduce(rmax[:, :], lg, AX.X, ALU.max))
                chain(nc.vector.tensor_tensor(shifted[:, :, :], lg, bc(rmax[:, :]), ALU.subtract))
                dve.wait_ge(s_exp, g + 1)
                chain(nc.vector.tensor_reduce(esum[:, :], expd[:, :, :], AX.X, ALU.add))
                chain(nc.vector.reciprocal(erec[:, :], esum[:, :]))
                chain(nc.vector.tensor_tensor(score[:, :, :], expd[:, :, :], bc(erec[:, :]), ALU.mult))
                nc.vector.memset(apart[:, :], 0.0)
                for t in range(TG):
                    last = nc.vector.max(top[:, t], score[:, t])
                chain(last)
                chain(nc.vector.memset(top[:, :, top_k:], 3.0))
                nc.vector.memset(apart[:, :], 0.0)
                for t in range(TG):
                    last = nc.vector.match_replace(left[:, t], top[:, t], score[:, t], -1.0)
                chain(last)
                chain(nc.vector.scalar_tensor_tensor(
                    chosen[:, :, :], left[:, :, :], 0.0, score[:, :, :], ALU.is_lt, ALU.mult))
                chain(nc.vector.tensor_reduce(wsum[:, :], chosen[:, :, :], AX.X, ALU.add))
                chain(nc.vector.tensor_scalar_add(wsum[:, :], wsum[:, :], 1e-20))
                chain(nc.vector.reciprocal(erec[:, :], wsum[:, :]))
                chain(nc.vector.tensor_tensor(comb[:, :, :], chosen[:, :, :], bc(erec[:, :]), ALU.mult))
                src = comb[:, :, :]
                for i in range(3):
                    chain(nc.vector.tensor_copy(part_b[:, :, :], src))
                    chain(nc.vector.tensor_copy(parts[:, :, i * E:(i + 1) * E], part_b[:, :, :]))
                    if i < 2:
                        chain(nc.vector.tensor_tensor(rest[:, i], src, part_b[:, :, :], ALU.subtract))
                        src = rest[:, i]
                assert step[0] == CHAIN
                dve.wait_ge(s_partsT, g + 1)
                nc.vector.tensor_copy(combT[:, :], ps_c[0][0:CE, :]).then_inc(s_combT, 1)
                for j in range(J):
                    dve.wait_ge(s_silu, g * J + (j + 1))
                    nc.vector.tensor_tensor(act[:, j % 2], act[:, j % 2], ps_u[j % 2][:, :], ALU.mult).then_inc(s_su, 1)
                    dve.wait_ge(s_su, g * J + (j + 1))
                    dve.wait_ge(s_c, g * J + (j + 1))
                    nc.vector.tensor_tensor(act[:, j % 2], act[:, j % 2], ps_c[j % 2][:, :], ALU.mult).then_inc(s_act, 1)
                    dve.wait_ge(s_act, g * J + (j + 1))
                    dve.wait_ge(s_ahi, g * J + (j + 1))
                    nc.vector.tensor_tensor(act_lo[:, j % 2], act[:, j % 2], act_hi[:, j % 2].bitcast(F32), ALU.subtract).then_inc(s_alo, 1)
                dve.wait_ge(s_down, g * J + J)
                for m in range(KC):
                    nc.vector.tensor_tensor(y_sb[:, m], ps_y[m][:, :], x_g[:, m], ALU.add).then_inc(s_y, 1)

        @block.tensor
        def _(pe):
            def cond(g):
                pe.wait_ge(s_z, g * KC + KC)
                for m in range(KC):
                    for k in range(KC):
                        last = nc.tensor.matmul(ps_g[m][:, :], w2c_sb[:, k, m * P:(m + 1) * P], z_g[:, k],
                                                start=(k == 0), stop=(k == KC - 1))
                last.then_inc(s_condps, 1)
                pe.wait_ge(s_hid, g * KC + KC)
                for t in range(TG):
                    for k in range(KC):
                        last = nc.tensor.matmul(ps_c[1][:, t * E:(t + 1) * E], hid[:, k, t * P:(t + 1) * P],
                                                gate_sb[:, k], start=(k == 0), stop=(k == KC - 1))
                last.then_inc(s_logit, 1)

            def transpose_parts(g):
                pe.wait_ge(s_r, g * CHAIN + CHAIN)
                pe.wait_ge(s_ones, 1)
                for t in range(TG):
                    last = nc.tensor.matmul(ps_c[0][0:CE, t * P:(t + 1) * P], parts[:, t], ident_sb[:, :],
                                            start=True, stop=True)
                last.then_inc(s_partsT, 1)

            def gate_up(g, j):
                if j == 0:
                    pe.wait_ge(s_hhi, g + 1)
                    pe.wait_ge(s_hlo, g + 1)
                pe.wait_ge(s_wsplit, 2 * j + 1)
                if j >= 2:
                    pe.wait_ge(s_silu, g * J + (j - 1))
                    pe.wait_ge(s_su, g * J + (j - 1))
                for h, bank in ((0, ps_g), (1, ps_u)):
                    n = 0
                    for k in range(KC):
                        for w, x in ((w13_hi, hid_hi), (w13_hi, hid_lo), (w13_lo, hid_hi)):
                            last = nc.tensor.matmul(bank[j % 2][:, :], w[:, j, k, h * P:(h + 1) * P], x[:, k],
                                                    start=(n == 0), stop=(n == 3 * KC - 1))
                            n += 1
                last.then_inc(s_gu, 1)

            def weight(g, j):
                if j == 0:
                    pe.wait_ge(s_combT, g + 1)
                if j >= 2:
                    pe.wait_ge(s_act, g * J + (j - 1))
                nc.tensor.matmul(ps_c[j % 2][:, :], sel_sb[:, j * P:(j + 1) * P], combT[:, :],
                                 start=True, stop=True).then_inc(s_c, 1)

            def down(g, j):
                pe.wait_ge(s_wsplit, 2 * j + 2)
                pe.wait_ge(s_ahi, g * J + (j + 1))
                pe.wait_ge(s_alo, g * J + (j + 1))
                for m in range(KC):
                    for i, (w, a) in enumerate(((w2_hi, act_hi), (w2_hi, act_lo), (w2_lo, act_hi))):
                        last = nc.tensor.matmul(ps_y[m][:, :], w[:, j, m * P:(m + 1) * P], a[:, j % 2],
                                                start=(j == 0 and i == 0), stop=(j == J - 1 and i == 2))
                last.then_inc(s_down, 1)

            pe.wait_ge(s_const, 16 * 8)
            for k in range(KC):
                last = nc.tensor.matmul(ps_c[0][:, k * B:(k + 1) * B], w3_sb[:, k * P:(k + 1) * P], q_sb[:, :],
                                        start=True, stop=True)
            last.then_inc(s_qps, 1)
            with pe.Fori(0, NG) as g:
                cond(g)
                gate_up(g, 0)
                gate_up(g, 1)
                transpose_parts(g)
                weight(g, 0)
                for j in range(J):
                    if j >= 1 and j + 1 < J:
                        gate_up(g, j + 1)
                    if j + 1 < J:
                        weight(g, j + 1)
                    down(g, j)


_OUT = ("out_0_dram", (128, 2, 2048))


def kernel(**inputs):
    import numpy as np
    import concourse.bacc as bacc
    from concourse.bass_utils import run_bass_kernel_spmd

    a = {k: np.asarray(v) for k, v in inputs.items()}
    x = a["x"]
    B, N, H = x.shape
    T, KC = B * N, H // P
    w13, w2, sw13, sw2 = (a["L0_ffn_" + n] for n in ("w13", "w2", "sw13", "sw2"))
    E, I = w13.shape[0], w13.shape[1] // 2
    IS = sw13.shape[0] // 2
    F = E * I + IS
    J = -(-F // P)
    up_down = np.zeros((3, J * P, H), np.float32)
    for n in range(2):
        up_down[n, :E * I] = w13[:, n * I:(n + 1) * I].reshape(E * I, H)
        up_down[n, E * I:F] = sw13[n * IS:(n + 1) * IS]
    up_down[2, :E * I] = w2.transpose(0, 2, 1).reshape(E * I, H)
    up_down[2, E * I:F] = sw2.T
    owner = np.minimum(np.arange(J * P) // I, E)
    sel = np.zeros((3 * E + 1, J * P), np.float32)
    for n in range(3):
        sel[n * E:(n + 1) * E] = owner[None, :] == np.arange(E)[:, None]
    sel[3 * E] = owner == E
    import ml_dtypes

    def chunks(m):
        return np.ascontiguousarray(m.reshape(KC, P, -1).transpose(1, 0, 2))

    w13T = up_down[:2].reshape(2, J, P, KC, P).transpose(1, 4, 3, 0, 2).reshape(J, P, KC, 2 * P)
    ins = {
        "xT": chunks(x.reshape(T, H).T),
        "qT": a["cond_1024"].T,
        "w3": a["L0_cond_W3"],
        "b3": a["L0_cond_b3"].reshape(KC, P).T,
        "w2c": chunks(a["L0_cond_W2"]),
        "b2": a["L0_cond_b2"].reshape(KC, P).T,
        "gateT": chunks(a["L0_ffn_gate_w"].T),
        "w13T": w13T,
        "w2T": up_down[2].reshape(J, P, H),
        "sel": sel.astype(ml_dtypes.bfloat16),
        "ident": np.eye(P, dtype=np.float32),
    }
    ins = {k: np.ascontiguousarray(v) for k, v in ins.items()}
    nc = bacc.Bacc("TRN2", target_bir_lowering=False, num_devices=1)
    aps = {k: nc.dram_tensor(k, v.shape, mybir.dt.from_np(v.dtype), kind="ExternalInput").ap() for k, v in ins.items()}
    aps["outT"] = nc.dram_tensor(_OUT[0], (P, KC, T), F32, kind="ExternalOutput").ap()
    adaln_moe_ffn(nc, top_k=6, **aps)
    r = run_bass_kernel_spmd(nc, [ins], core_ids=[0])
    out = r.results[0][_OUT[0]]
    return out.transpose(2, 1, 0).reshape(B, N, H)
```

```python
from contextlib import ExitStack

import concourse.bass as bass
from concourse import mybir
from concourse.alu_op_type import AluOpType as ALU

P = 128
F32 = mybir.dt.float32
F32R = mybir.dt.float32r
BF16 = mybir.dt.bfloat16
F16 = mybir.dt.float16
I32 = mybir.dt.int32
U32 = mybir.dt.uint32
ACT = mybir.ActivationFunctionType
AX = mybir.AxisListType

RING = 4
LAG = 6
AHEAD = 3


def reuse(eng, sem, value):
    if not (isinstance(value, int) and value <= 0):
        eng.wait_ge(sem, value)


def adaln_moe_ffn(nc, x_rows, xT, qT, w3, b3, w2c, b2, gateT, w13T, w2T, sw13T, sw2T,
                  ident, tri, ones, iota_e, iota_k, iota_p, token1, out, top_k):
    T, H = x_rows.shape
    KC = H // P
    B = qT.shape[1]
    N = T // B
    E = gateT.shape[2]
    I2 = w13T.shape[3]
    I = I2 // 2
    IC = I // KC
    SJ = sw2T.shape[1]
    GT = 512
    NG = T // GT
    BG = GT // N
    TG = GT // P
    TT = T // P
    TK = TT * top_k
    NT = -(-(TK + E - 1) // RING) * RING
    EARLY = NG // 2
    W = H + 2 * top_k
    assert NT <= P

    hid_dram = nc.dram_tensor("hid_rows", (T, W), F32, kind="Internal").ap()
    sums = [nc.dram_tensor(f"sum{i}", (T + P, H), F32, kind="Internal").ap() for i in range(2)]
    late_dram = nc.dram_tensor("late_hid", (NG - EARLY, P, KC, GT), F32, kind="Internal").ap()

    with ExitStack() as ctx:
        def sb(name, shape, dt=F32):
            return ctx.enter_context(nc.sbuf_tensor(name, shape, dt))

        def sem(name):
            return ctx.enter_context(nc.semaphore(name))

        w13_hi = sb("w13_hi", [P, E, KC, I2], F32R)
        w13_lo = sb("w13_lo", [P, E, KC, I2], F32R)
        w2_hi = sb("w2_hi", [IC, E, KC, H], F32R)
        w2_lo = sb("w2_lo", [IC, E, KC, H], F32R)
        sw13 = sb("sw13", [P, KC, 2, SJ * P])
        sw2 = sb("sw2", [P, SJ, H])
        xg = sb("x_gathered", [P, RING, W])
        x_hi = sb("x_hi", [P, 2, KC * P], F32R)
        x_lo = sb("x_lo", [P, 2, KC * P], F32R)
        sil_h = sb("silu_and_h", [P, 4, I])
        sil, hid_e = sil_h[:, 0:2], sil_h[:, 2:4]
        a_hi = sb("a_hi", [IC, 2, KC * P], F32R)
        a_lo = sb("a_lo", [IC, 2, KC * P], F32R)
        y_sb = sb("y_sb", [P, RING, H])
        gidx = sb("gather_index", [P, RING], U32)
        sidx = sb("scatter_index", [P, RING], U32)
        EL = 2
        SEL = TK * E
        R_END = GT * KC + SEL
        arena = sb("arena", [P, max(R_END + EARLY * KC * GT + TG * H, (NG + 3) * TG * H)])
        at = [0]

        def carve(n, start=None):
            a = at[0] if start is None else start
            at[0] = a + n
            return arena[:, a:a + n]

        x_g = [carve(KC * GT).rearrange("p (k n) -> p k n", k=KC) for _ in range(2)]
        LATE_X = E - -(-(NG - 2) * KC * GT // (KC * I2))
        x_late = w13_hi[:, LATE_X:].rearrange("p e k n -> p (e k n)").bitcast(F32)
        x_g += [x_late[:, g * KC * GT:(g + 1) * KC * GT].rearrange("p (k n) -> p k n", k=KC) for g in range(NG - 2)]
        w2c_sb = carve(KC * H).rearrange("p (k n) -> p k n", k=KC)
        assert at[0] <= R_END
        act_f = carve(2 * GT, 0).rearrange("p (b n) -> p b n", b=2)
        sel = carve(SEL)
        early = [carve(KC * GT) for _ in range(EARLY)]
        rows = carve(TG * H)
        hid = [h.rearrange("p (k n) -> p k n", k=KC) for h in early]
        hid += [b[:, :, :].rearrange("p r n -> p (r n)")[:, 0:KC * GT].rearrange("p (k n) -> p k n", k=KC)
                for b in (xg, y_sb)]
        base = [h.rearrange("p (t n) -> p t n", t=TG) for h in early]
        rows4 = rows.rearrange("p (t n) -> p t n", t=TG)
        x_free = x_g[0].rearrange("p k n -> p (k n)")
        rows_g = [x_free.rearrange("p (t n) -> p t n", t=TG), rows4]
        OHL, OHH = P * top_k // 2, NT * top_k // 2
        iota_k_sb = carve(OHL).bitcast(F16).rearrange("p (n k) -> p n k", k=top_k)
        oh = [sel[:, 0:OHL + 2 * OHH], carve(OHL + 2 * OHH)]
        lo1 = [b[:, 0:OHL].bitcast(F16).rearrange("p (n k) -> p n k", k=top_k) for b in oh]
        hi1 = [b[:, OHL:OHL + OHH].bitcast(F16).rearrange("p (n k) -> p n k", k=top_k) for b in oh]
        hi_tok = [b[:, OHL + OHH:].bitcast(F16).rearrange("p (n k) -> p n k", k=top_k) for b in oh]
        assert at[0] <= (NG + 3) * TG * H
        def sums_of_group(a):
            return a.rearrange("p (t n) -> p t n", t=TG)

        hid_l = [carve(KC * GT, g * KC * GT).rearrange("p (k n) -> p k n", k=KC) for g in range(NG - EARLY)]
        sum_a = [sums_of_group(carve(TG * H)) for _ in range(NG - 1)]
        sum_a.append(y_sb[:, :, :])
        sum_b = [sums_of_group(carve(TG * H)) for _ in range(2)]
        act_l = xg[:, :, :].rearrange("p r n -> p (r n)")[:, 0:2 * GT].rearrange("p (b n) -> p b n", b=2)
        def r_words(a, n):
            return oh[1][:, a:a + n]
        TE = TT * E
        shifted = r_words(0, TE).rearrange("p (t e) -> p t e", e=E)
        expd = r_words(TE, TE).rearrange("p (t e) -> p t e", e=E)
        score = r_words(2 * TE, TE).rearrange("p (t e) -> p t e", e=E)
        slot_te = r_words(0, TE).rearrange("p (t e) -> p t e", e=E)
        top = r_words(3 * TE, TT * 8).rearrange("p (t k) -> p t k", k=8)
        topi = r_words(3 * TE + TT * 8, TT * 8).bitcast(U32).rearrange("p (t k) -> p t k", k=8)
        w_tok = sb("w_tok", [P, TT, 2, top_k])
        rsmall = sb("rsmall", [P, 3, TT])
        slot = sb("slot", [P, TK])
        slot_i = r_words(TE, 2 * TK).bitcast(I32).rearrange("p (v n) -> p v n", v=2)
        slot_lo = sb("slot_lo", [P, TK], F16)
        slot_hi = sb("slot_hi", [P, TK], F16)
        mask = sb("mask", [P, TT + 1, E], BF16)
        esm = sb("esm", [P, 6, E])
        esi = sb("esi", [P, 2, E], I32)
        te_p = sb("te_p", [P, 1])
        te_diag = sb("te_diag", [P, P], BF16)
        te_all = sb("te_all", [P, NT])
        te = sb("te", [1, NT + 2 * RING], I32)
        idx_f = r_words(TE, NT)
        idx_t = r_words(2 * TE, NT)
        g_all = sb("g_all", [P, NT], U32)
        s_all = sb("s_all", [P, NT], U32)
        w_pick = sb("w_pick", [P, RING, top_k])
        w_slot = sb("w_slot", [P, RING])
        past_end = sb("past_end", [P, 1])
        ident_sb = sb("ident_sb", [P, P])
        tri_sb = sb("tri_sb", [P, P], BF16)
        ones_sb = sb("ones_sb", [P, P], BF16)
        iota_e_sb = sb("iota_e_sb", [P, E])
        iota_p_sb = sb("iota_p_sb", [P, 1])
        token1_sb = sb("token1_sb", [P, TT])
        q_sb = sb("q_sb", [P, B])
        w3_sb = sil_h[:, 0:2].rearrange("p a n -> p (a n)")[:, 0:H]
        vsum = sil_h[:, 2:4].rearrange("p a n -> p (a n)")[:, 0:2 * KC * BG].rearrange("p (b k n) -> p b k n", b=2, k=KC)
        qemb = sb("qemb", [P, KC, B])
        b3_sb = sb("b3_sb", [P, KC])
        b2_sb = sb("b2_sb", [P, KC])
        gate_sb = sb("gate_sb", [P, KC, E])
        zeros_h = sb("zeros_h", [P, P], F16)
        assert OHL + 2 * OHH + H <= SEL
        zero_row = sel[:, SEL - H:]

        gu_x = ctx.enter_context(nc.psum_tensor("gu_x", [P, 4, GT], F32))
        h_y = ctx.enter_context(nc.psum_tensor("h_y", [P, 4, GT], F32))
        ps_gu, ps_x = [gu_x[:, 0], gu_x[:, 1]], [gu_x[:, 2], gu_x[:, 3]]
        ps_h, ps_y = [h_y[:, 0], h_y[:, 1]], [h_y[:, 2], h_y[:, 3]]
        ps_rank, ps_logit, ps_idx = ps_h[0], ps_h[1], ps_h[1]

        s_q = sem("q_loaded")
        s_c1 = sem("w2c_gate_loaded")
        s_c2 = sem("constants_loaded")
        s_sw = sem("shared_weights_loaded")
        s_xin = [sem(f"x_group_loaded{g}") for g in range(NG)]
        s_raw = [sem(f"expert_weights_loaded{i}") for i in range(E // EL)]
        s_whi = sem("weights_hi")
        s_wlo = sem("weights_lo")
        s_qps = sem("qemb_in_psum")
        s_qemb = sem("qemb_ready")
        s_z = sem("z_ready")
        s_cond = sem("cond_in_psum")
        s_hid = sem("hid_ready")
        s_gate = sem("logits_in_psum")
        s_tr = sem("hid_transposed")
        s_row = sem("hid_rows_ready")
        s_rowst = [sem(f"hid_rows_stored{i}") for i in range(2)]
        s_late = sem("late_hid_stored")
        s_v = sem("vector_step")
        s_exp = sem("exp_ready")
        s_mask = sem("mask_ready")
        s_rank = sem("ranks_in_psum")
        s_tep = sem("tile_expert_column_ready")
        s_teps = sem("tile_expert_row_in_psum")
        s_te = sem("tile_expert_ready")
        s_hi1 = sem("tile_one_hots_ready")
        s_oh = sem("place_one_hots_ready")
        s_hit = sem("token_one_hots_ready")
        s_idxmm = sem("one_hots_used")
        s_idxps = sem("indices_in_psum")
        s_idx = sem("indices_ready")
        s_zero = sem("zeros_set")
        s_sgu = sem("shared_gate_up_in_psum")
        s_ssil = sem("shared_silu_ready")
        s_smul = sem("shared_act_ready")
        s_sdown = sem("shared_down_done")
        s_sum0 = sem("sums_initialised")
        s_wst = sem("weights_stored")
        s_w = sem("weights_ready")
        s_base = sem("base_ready")
        s_basest = sem("base_stored")
        s_gi = sem("gather_index_ready")
        s_xgin = [sem(f"x_gathered{i}") for i in range(RING)]
        s_t1 = sem("x_transposed")
        s_xhi = sem("x_hi_ready")
        s_xlo = sem("x_lo_ready")
        s_gu = sem("gate_up_in_psum")
        s_sil = sem("silu_ready")
        s_h = sem("h_ready")
        s_t2 = sem("h_transposed")
        s_ahi = sem("a_hi_ready")
        s_alo = sem("a_lo_ready")
        s_yps = sem("y_in_psum")
        s_yout = sem("y_ready")
        s_scat = [sem(f"y_scattered{i}") for i in range(RING)]
        s_carry = sem("carries_a_wait")
        s_hl = sem("late_hid_loaded")
        s_suma = [sem(f"sum_loaded{g}") for g in range(NG)]
        s_add = sem("sums_added")
        s_done = sem("late_half_done")
        s_out = sem("out_stored")

        block = ctx.enter_context(nc.Block())

        def steps(eng, body, last, begin=None):
            rounds = range(-(-last // RING))
            for q in rounds[:1]:
                args = (begin(q),) if begin else ()
                for r in range(RING):
                    body(q * RING + r, r, q, *args)
            with eng.Fori(1, NT // RING) as q:
                args = (begin(q),) if begin else ()
                for r in range(RING):
                    body(q * RING + r, r, q, *args)
            for q in rounds[NT // RING:]:
                args = (begin(q),) if begin else ()
                for r in range(last - q * RING):
                    body(q * RING + r, r, q, *args)

        def live(t):
            return not isinstance(t, int) or 0 <= t < NT

        assert EARLY == 2 and SJ == 3 and TT == 16

        def pair(body, q):
            for b in range(2):
                body(2 * q + b, b)

        PIECES = [(e, part) for e in range(E) for part in range(2)]

        def split_piece(w13, w2, n):
            e, part = PIECES[n]
            return w13[:, e] if part == 0 else w2[:, e]

        @block.sync
        def _(sp):
            sp.dma_start(x_g[0], xT[:, :, 0:GT]).then_inc(s_xin[0], 16)
            sp.dma_start(q_sb[:, :], qT).then_inc(s_q, 16)
            sp.dma_start(w3_sb, w3).then_inc(s_q, 16)
            sp.dma_start(b3_sb[:, :], b3).then_inc(s_q, 16)
            sp.dma_start(w2c_sb, w2c).then_inc(s_c1, 16)
            sp.dma_start(b2_sb[:, :], b2).then_inc(s_c1, 16)
            sp.dma_start(x_g[1], xT[:, :, GT:2 * GT]).then_inc(s_xin[1], 16)
            sp.dma_start(gate_sb[:, :, :], gateT).then_inc(s_c1, 16)
            for g in range(2, NG):
                sp.dma_start(x_g[g], xT[:, :, g * GT:(g + 1) * GT]).then_inc(s_xin[g], 16)

            def load_weights(i):
                for lo, w in ((w13_lo, w13T), (w2_lo, w2T)):
                    sp.dma_start(lo[:, i * EL:(i + 1) * EL].bitcast(F32),
                                 w[i * EL:(i + 1) * EL].rearrange("e k p n -> p e k n")).then_inc(s_raw[i], 16)

            load_weights(0)
            for dst, src in ((ident_sb, ident), (tri_sb, tri), (ones_sb, ones), (iota_e_sb, iota_e),
                             (iota_p_sb, iota_p), (token1_sb, token1)):
                sp.dma_start(dst[:, :], src).then_inc(s_c2, 16)
            sp.dma_start(iota_k_sb, iota_k).then_inc(s_c2, 16)
            for i in range(1, E // EL):
                if i > 2:
                    sp.wait_ge(s_whi, 2 * EL * (i - 2))
                load_weights(i)
                if i == 3:
                    sp.dma_start(sw13[:, :, :, :], sw13T).then_inc(s_sw, 16)
                    sp.dma_start(sw2[:, :, :], sw2T).then_inc(s_sw, 16)

            def rows_of(dram, g):
                return dram[g * GT:(g + 1) * GT, :].rearrange("(t p) n -> p t n", p=P)

            sp.dma_start(sums[0][T:T + P, :], x_rows[0:P, :]).then_inc(s_sum0, 16)
            sp.dma_start(sums[1][T:T + P, :], x_rows[0:P, :]).then_inc(s_sum0, 16)
            for g in range(NG):
                sp.dma_start(sums[0][g * GT:(g + 1) * GT, :], x_rows[g * GT:(g + 1) * GT, :]).then_inc(s_sum0, 16)
            sp.wait_ge(s_w, 1)
            sp.dma_start(hid_dram[:, H:W].rearrange("(t p) k -> p t k", p=P),
                         w_tok[:, :, :, :].rearrange("p t a k -> p t (a k)")).then_inc(s_wst, 16)
            sp.wait_ge(s_zero, 3)
            for g in range(EARLY, NG):
                sp.dma_start(rows_of(sums[1], g), zero_row.unsqueeze(1).to_broadcast([P, TG, H])).then_inc(s_sum0, 16)
            for g in range(EARLY):
                sp.wait_ge(s_base, (g + 1) * 2)
                sp.dma_start(rows_of(sums[1], g), base[g]).then_inc(s_basest, 16)
            sp.wait_ge(s_basest, 16 * EARLY)
            sp.wait_ge(s_late, 16 * (NG - EARLY))
            sp.wait_ge(s_sum0, 16 * (2 + NG + NG - EARLY))
            sp.wait_ge(s_yout, LAG + 1)
            for g in range(NG - EARLY):
                sp.dma_start(hid_l[g], late_dram[g]).then_inc(s_hl, 16)
            for r in range(RING):
                sp.wait_ge(s_scat[r], 16 * (NT // RING))

            def store_out(g):
                sp.wait_ge(s_add, g + 1)
                sp.dma_start(rows_of(out, g), sum_a[g]).then_inc(s_out, 16)

            for g in range(NG):
                if g >= 2:
                    store_out(g - 2)
                sp.dma_start(sum_a[g], rows_of(sums[0], g)).then_inc(s_suma[g], 16)
                sp.dma_start(sum_b[g % 2], rows_of(sums[1], g)).then_inc(s_suma[g], 16)
            for g in range(EARLY, NG):
                for b in range(2):
                    sp.wait_ge(s_done, 2 * (g - EARLY) + b + 1)
                    at_t = g * GT + b * GT // 2
                    sp.dma_start(out[at_t:at_t + GT // 2, :].rearrange("(t p) n -> p t n", p=P),
                                 sum_a[g][:, 2 * b:2 * b + 2, :]).then_inc(s_out, 16)
            sp.wait_ge(s_out, 16 * (EARLY + 2 * (NG - EARLY)))

        @block.gpsimd
        def _(pool):
            for n in range(len(PIECES)):
                pool.wait_ge(s_whi, n + 1)
                lo = split_piece(w13_lo, w2_lo, n)
                nc.gpsimd.tensor_sub(lo, lo.bitcast(F32), split_piece(w13_hi, w2_hi, n).bitcast(F32)).then_inc(s_wlo, 1)
            for b in range(2):
                pool.wait_ge(s_rowst[b], 16 * (NG // 2))
            pool.wait_ge(s_wst, 16)
            pool.wait_ge(s_late, 16 * (NG - EARLY))

            def step(s, r, q):
                if live(s):
                    pool.wait_ge(s_gi, s + 1)
                    pool.sem_inc(s_carry, 1)
                    nc.gpsimd.indirect_dma_start(
                        out=xg[:, r, :], out_offset=None, in_=hid_dram,
                        in_offset=bass.IndirectOffsetOnAxis(ap=gidx[:, r:r + 1], axis=0),
                        bounds_check=T - 1, oob_is_err=True).then_inc(s_xgin[r], 16)
                t, rt = s - LAG, (r - LAG) % RING
                if isinstance(t, int) and t == 0:
                    pool.wait_ge(s_sum0, 16 * (2 + NG + NG - EARLY))
                    pool.wait_ge(s_basest, 16 * EARLY)
                if live(t):
                    pool.wait_ge(s_yout, s + 1)
                    reuse(pool, s_scat[(rt - 2) % RING], 16 * (q + (r - LAG - 2) // RING + 1))
                    pool.sem_inc(s_carry, 1)
                    nc.gpsimd.indirect_dma_start(
                        out=sums[r % 2], out_offset=bass.IndirectOffsetOnAxis(ap=sidx[:, rt:rt + 1], axis=0),
                        in_=y_sb[:, rt, :], in_offset=None, compute_op=ALU.add,
                        bounds_check=T + P - 1, oob_is_err=True).then_inc(s_scat[rt], 16)

            for s in range(3 * RING):
                step(s, s % RING, s // RING)
            with pool.Fori(3, NT // RING) as q:
                for r in range(RING):
                    step(q * RING + r, r, q)
            for s in range(NT, NT + LAG):
                step(s, s % RING, s // RING)
            for r in range(RING):
                pool.wait_ge(s_scat[r], 16 * (NT // RING))

        def shared_act(n):
            return (act_f if n < EARLY * SJ else act_l)[:, n % 2]

        SHIFTED = 3 * NG + 2

        @block.scalar
        def _(act):
            split = [0]

            def split_hi(count):
                for _ in range(count):
                    n = split[0]
                    if n < len(PIECES):
                        act.wait_ge(s_raw[PIECES[n][0] // EL], 32)
                        nc.scalar.activation(split_piece(w13_hi, w2_hi, n), split_piece(w13_lo, w2_lo, n).bitcast(F32),
                                             ACT.Copy).then_inc(s_whi, 1)
                        split[0] += 1

            act.wait_ge(s_qps, 1)
            for k in range(KC):
                last = nc.scalar.activation(qemb[:, k], ps_h[0][:, k * B:(k + 1) * B], ACT.Relu, bias=b3_sb[:, k:k + 1])
            last.then_inc(s_qemb, 1)

            def to_rows(g):
                if g >= 2:
                    act.wait_ge(s_rowst[g % 2], 16 * (g // 2))
                for i in range(TG):
                    act.wait_ge(s_tr, g * TG + i + 1)
                    nc.scalar.activation(rows_g[g % 2][:, i], ps_x[i % 2][:, 0:H], ACT.Copy).then_inc(s_row, 1)
                act.wait_ge(s_row, (g + 1) * TG)
                act.dma_start(hid_dram[g * GT:(g + 1) * GT, 0:H].rearrange("(t p) n -> p t n", p=P),
                              rows_g[g % 2]).then_inc(s_rowst[g % 2], 16)

            act.wait_ge(s_c1, 16 * 3)
            for g in range(NG):
                act.wait_ge(s_cond, g + 1)
                bank = ps_gu if g % 2 == 0 else ps_y
                for m in range(KC):
                    nc.scalar.activation(hid[g][:, m], bank[m], ACT.Relu, bias=b2_sb[:, m:m + 1]).then_inc(s_hid, 1)
                if g >= EARLY:
                    act.wait_ge(s_hid, (g + 1) * KC)
                    act.dma_start(late_dram[g - EARLY], hid[g]).then_inc(s_late, 16)
                if g:
                    to_rows(g - 1)
                split_hi(4 if g < NG - 1 else 2)
            assert 2 * LATE_X >= split[0]

            def shared_silu(n):
                act.wait_ge(s_sgu, n + 1)
                reuse(act, s_sdown, n - 1)
                nc.scalar.activation(shared_act(n), gu_x[:, 2 * (n % 2)], ACT.Silu).then_inc(s_ssil, 1)

            def base_copy(g):
                act.wait_ge(s_sdown, (g + 1) * SJ)
                for b in range(2):
                    v = base[g][:, 2 * b:2 * b + 2, :].rearrange("p t n -> p (t n)")
                    nc.scalar.activation(v, ps_y[b], ACT.Copy).then_inc(s_base, 1)

            def scale_one_hots(t, b):
                tok = slice(t, t + 1)
                reuse(act, s_idxmm, t - 1)
                act.wait_ge(s_hi1, t + 1)
                nc.scalar.activation(hi_tok[b], hi1[b], ACT.Copy, scale=token1_sb[:, tok]).then_inc(s_hit, 1)

            act.wait_ge(s_v, SHIFTED)
            nc.scalar.activation(expd, shifted, ACT.Exp).then_inc(s_exp, 1)
            to_rows(NG - 1)
            act.wait_ge(s_rowst[0], 16 * (NG // 2))
            shared_silu(0)
            split_hi(6)
            shared_silu(1)
            split_hi(6)
            shared_silu(2)
            split_hi(6)
            assert split[0] == len(PIECES)
            pair(scale_one_hots, 0)
            shared_silu(3)
            for q in range(1, 4):
                pair(scale_one_hots, q)
            base_copy(0)
            pair(scale_one_hots, 4)
            shared_silu(4)
            for q in range(5, TT // 2):
                pair(scale_one_hots, q)
            shared_silu(5)
            base_copy(1)

            def step(s, r, q):
                if live(s):
                    act.wait_ge(s_t1, s + 1)
                    nc.scalar.activation(x_hi[:, r % 2], ps_x[r % 2][:, 0:KC * P], ACT.Copy).then_inc(s_xhi, 1)
                if live(s - 1):
                    act.wait_ge(s_gu, s + 1)
                    nc.scalar.activation(sil[:, (r - 1) % 2], ps_gu[(r - 1) % 2][:, 0:I], ACT.Silu).then_inc(s_sil, 1)
                if live(s - 2):
                    act.wait_ge(s_t2, s + 1)
                    nc.scalar.activation(a_hi[:, r % 2], ps_h[r % 2][0:IC, 0:KC * P], ACT.Copy).then_inc(s_ahi, 1)

            act.sem_inc(s_sil, 1)
            act.sem_inc(s_ahi, 2)
            steps(act, step, NT + 3)
            for n in range(EARLY * SJ, NG * SJ):
                shared_silu(n)

        @block.vector
        def _(dve):
            count = [0]

            def chain(ins):
                count[0] += 1
                ins.then_inc(s_v, 1)
                dve.wait_ge(s_v, count[0])

            nc.vector.memset(zeros_h[:, :], 0.0)
            nc.vector.memset(te[:, :], 0).then_inc(s_zero, 1)
            nc.vector.memset(mask[:, TT, :], 0.0).then_inc(s_zero, 1)
            for g in range(NG):
                dve.wait_ge(s_xin[g], 16)
                x4 = x_g[g].rearrange("p k (b n) -> p k b n", n=N)
                chain(nc.vector.tensor_reduce(vsum[:, g % 2], x4, AX.X, ALU.add))
                for k in range(KC):
                    last = nc.vector.scalar_tensor_tensor(
                        x4[:, k], x4[:, k], float(N), vsum[:, g % 2, k, :].unsqueeze(2).to_broadcast([P, BG, N]),
                        ALU.mult, ALU.add)
                chain(last)
                if g == 0:
                    dve.wait_ge(s_qemb, 1)
                for k in range(KC):
                    last = nc.vector.tensor_tensor(
                        x4[:, k], x4[:, k],
                        qemb[:, k, g * BG:(g + 1) * BG].unsqueeze(2).to_broadcast([P, BG, N]), ALU.mult)
                last.then_inc(s_z, 1)
                count[0] += 1
                nc.vector.sem_inc(s_v, 1)

            def per_tile(a):
                return a.unsqueeze(2).to_broadcast([P, TT, E])

            def shared_mul(n):
                dve.wait_ge(s_ssil, n + 1)
                a = shared_act(n)
                nc.vector.tensor_tensor(a, a, gu_x[:, 2 * (n % 2) + 1], ALU.mult).then_inc(s_smul, 1)

            rmax, esum, rec = (rsmall[:, n, :] for n in range(3))
            lg = ps_logit[:, 0:TE].rearrange("p (t e) -> p t e", e=E)
            dve.wait_ge(s_gate, NG)
            dve.wait_ge(s_c2, 16 * 7)
            chain(nc.vector.tensor_reduce(rmax, lg, AX.X, ALU.max))
            chain(nc.vector.tensor_tensor(shifted, lg, per_tile(rmax), ALU.subtract))
            assert count[0] == SHIFTED
            dve.wait_ge(s_exp, 1)
            chain(nc.vector.tensor_reduce(esum, expd, AX.X, ALU.add))
            chain(nc.vector.reciprocal(rec, esum))
            chain(nc.vector.tensor_tensor(score, expd, per_tile(rec), ALU.mult))
            for t in range(TT):
                last = nc.vector.max(top[:, t], score[:, t])
            chain(last)
            for t in range(TT):
                last = nc.vector.max_index(topi[:, t], top[:, t], score[:, t])
            chain(last)
            eidx = w_tok[:, :, 1]
            chain(nc.vector.tensor_copy(eidx, topi[:, :, 0:top_k]))
            sel_v = sel.rearrange("p (j e) -> p j e", e=E)
            sel4 = sel.rearrange("p (t k e) -> p t k e", k=top_k, e=E)
            chain(nc.vector.tensor_tensor(sel4, eidx.unsqueeze(3).to_broadcast([P, TT, top_k, E]),
                                          iota_e_sb[:, :].unsqueeze(1).unsqueeze(1).to_broadcast([P, TT, top_k, E]),
                                          ALU.is_equal))
            with nc.allow_low_precision("a mask of zeros and ones"):
                nc.vector.tensor_reduce(mask[:, 0:TT, :], sel.rearrange("p (t k e) -> p t e k", k=top_k, e=E),
                                        AX.X, ALU.add).then_inc(s_mask, 1)
            shared_mul(0)
            chain(nc.vector.tensor_reduce(esum, top[:, :, 0:top_k], AX.X, ALU.add))
            chain(nc.vector.tensor_scalar_add(rmax, esum, 1e-20))
            chain(nc.vector.reciprocal(rec, rmax))
            chain(nc.vector.tensor_tensor(w_tok[:, :, 0], top[:, :, 0:top_k],
                                          rec.unsqueeze(2).to_broadcast([P, TT, top_k]), ALU.mult))
            nc.vector.sem_inc(s_w, 1)

            shared_mul(1)
            tiles, ends, begin, zero, le = (esm[:, n, :] for n in range(5))
            dve.wait_ge(s_rank, 1)
            chain(nc.vector.tensor_scalar(esi[:, 0, :], ps_rank[:, TE:TE + E], float(P - 1), None, ALU.add))
            chain(nc.vector.tensor_scalar(esi[:, 1, :], esi[:, 0, :], 7, None, ALU.arith_shift_right))
            nc.vector.memset(zero, 0.0)
            chain(nc.vector.tensor_copy(tiles, esi[:, 1, :]))
            chain(nc.vector.tensor_tensor_scan(ends, tiles, zero, 0.0, ALU.add, ALU.add))
            chain(nc.vector.tensor_tensor(begin, ends, tiles, ALU.subtract))
            chain(nc.vector.tensor_scalar(begin, begin, float(P), None, ALU.mult))
            chain(nc.vector.tensor_tensor(slot_te, ps_rank[:, 0:TE].rearrange("p (t e) -> p t e", e=E),
                                          begin.unsqueeze(1).to_broadcast([P, TT, E]), ALU.add))
            chain(nc.vector.tensor_scalar(le, ends, iota_p_sb[:, 0:1], None, ALU.is_le))
            chain(nc.vector.tensor_reduce(te_p[:, :], le, AX.X, ALU.add))
            chain(nc.vector.tensor_scalar_min(te_p[:, :], te_p[:, :], float(E - 1)))
            nc.vector.tensor_scalar(te_diag[:, :], ident_sb[:, :], te_p[:, 0:1], None, ALU.mult).then_inc(s_tep, 1)
            for k in range(top_k):
                last = nc.vector.tensor_tensor(sel4[:, :, k], sel4[:, :, k], slot_te, ALU.mult)
            chain(last)
            chain(nc.vector.tensor_reduce(slot[:, :], sel_v, AX.X, ALU.add))
            chain(nc.vector.tensor_copy(slot_i[:, 0, :], slot[:, :]))
            chain(nc.vector.tensor_scalar(slot_i[:, 1, :], slot_i[:, 0, :], P - 1, None, ALU.bitwise_and))
            chain(nc.vector.tensor_copy(slot_lo[:, :], slot_i[:, 1, :]))
            chain(nc.vector.tensor_scalar(slot_i[:, 1, :], slot_i[:, 0, :], 7, None, ALU.arith_shift_right))
            chain(nc.vector.tensor_copy(slot_hi[:, :], slot_i[:, 1, :]))
            def one_hots(t, b):
                of_tile = slice(t * top_k, (t + 1) * top_k)
                for dst, of_slot, n, ready, read in ((hi1[b], slot_hi, NT, s_hi1, s_hit), (lo1[b], slot_lo, P, s_oh, s_idxmm)):
                    reuse(dve, read, t - 1)
                    nc.vector.tensor_tensor(dst, iota_k_sb[:, 0:n],
                                            of_slot[:, of_tile].unsqueeze(1).to_broadcast([P, n, top_k]),
                                            ALU.is_equal).then_inc(ready, 1)

            shared_mul(2)
            pair(one_hots, 0)
            dve.wait_ge(s_teps, 1)
            nc.vector.tensor_copy(te[:, 3:3 + NT], ps_rank[0:1, 0:NT]).then_inc(s_te, 1)
            nc.vector.tensor_copy(te_all[:, :], ps_rank[:, 0:NT])
            nc.vector.memset(zero_row, 0.0).then_inc(s_zero, 1)
            pair(one_hots, 1)
            shared_mul(3)
            for q in range(2, 6):
                pair(one_hots, q)
            shared_mul(4)
            for q in range(6, TT // 2):
                pair(one_hots, q)

            def gather_index(s, r):
                col = slice(s, s + 1) if isinstance(s, int) else bass.ds(s, 1)
                nc.vector.tensor_copy(gidx[:, r:r + 1], g_all[:, col]).then_inc(s_gi, 1)

            dve.wait_ge(s_idxps, 1)
            chain(nc.vector.tensor_copy(idx_f, ps_idx[:, 0:NT]))
            chain(nc.vector.tensor_scalar(g_all[:, :], idx_f, -1.0, 0.0, ALU.add, ALU.max))
            dve.wait_ge(s_late, 16 * (NG - EARLY))
            for s in range(AHEAD):
                gather_index(s, s)
            chain(nc.vector.tensor_scalar(past_end[:, :], iota_p_sb[:, 0:1], float(T + 1), None, ALU.add))
            chain(nc.vector.tensor_scalar(idx_t, idx_f, 0.0, past_end[:, 0:1], ALU.is_equal, ALU.mult))
            chain(nc.vector.scalar_tensor_tensor(s_all[:, :], idx_f, -1.0, idx_t, ALU.add, ALU.add))

            shared_mul(5)

            def step(s, r, q):
                if live(s):
                    dve.wait_ge(s_xhi, s + 1)
                    col = slice(s, s + 1) if isinstance(s, int) else bass.ds(s, 1)
                    nc.vector.scalar_tensor_tensor(w_pick[:, r], xg[:, r, H + top_k:W], te_all[:, col],
                                                   xg[:, r, H:H + top_k],
                                                   ALU.is_equal, ALU.mult, accum_out=w_slot[:, r:r + 1])
                    nc.vector.tensor_tensor(x_lo[:, r % 2], ps_x[r % 2][:, 0:KC * P], x_hi[:, r % 2].bitcast(F32),
                                            ALU.subtract).then_inc(s_xlo, 1)
                if not isinstance(s, int) or s + AHEAD < NT:
                    gather_index(s + AHEAD, (r + AHEAD) % RING)
                if live(s - 1):
                    b = (r - 1) % 2
                    dve.wait_ge(s_sil, s + 1)
                    nc.vector.scalar_tensor_tensor(hid_e[:, b], sil[:, b], w_slot[:, (r - 1) % RING:(r - 1) % RING + 1], ps_gu[b][:, I:I2],
                                                   ALU.mult, ALU.mult).then_inc(s_h, 1)
                if live(s - 2):
                    dve.wait_ge(s_ahi, s + 1)
                    nc.vector.tensor_tensor(a_lo[:, r % 2], ps_h[r % 2][0:IC, 0:KC * P], a_hi[:, r % 2].bitcast(F32),
                                            ALU.subtract).then_inc(s_alo, 1)
                if live(s - 3):
                    rt = (r - 3) % RING
                    reuse(dve, s_scat[rt], 16 * (q + (r - 3) // RING))
                    t = s - 3
                    col = slice(t, t + 1) if isinstance(t, int) else bass.ds(t, 1)
                    nc.vector.tensor_copy(sidx[:, rt:rt + 1], s_all[:, col])
                    dve.wait_ge(s_yps, s + 1)
                    nc.vector.tensor_copy(y_sb[:, rt], ps_y[rt % 2][:, 0:H]).then_inc(s_yout, 1)

            dve.sem_inc(s_xlo, 1)
            dve.sem_inc(s_h, 2)
            dve.sem_inc(s_alo, 3)
            dve.sem_inc(s_yout, LAG)
            for s in range(2 * RING):
                step(s, s % RING, s // RING)
            with dve.Fori(2, NT // RING - 1) as q:
                for r in range(RING):
                    step(q * RING + r, r, q)
            for s in range(NT - RING, NT + 3):
                step(s, s % RING, s // RING)

            def add_sums(g):
                dve.wait_ge(s_suma[g], 32)
                nc.vector.tensor_tensor(sum_a[g], sum_a[g], sum_b[g % 2], ALU.add).then_inc(s_add, 1)

            for i in range(NG - EARLY):
                for j in range(SJ):
                    n = (EARLY + i) * SJ + j
                    shared_mul(n)
                    if n - EARLY * SJ < NG:
                        add_sums(n - EARLY * SJ)
                dve.wait_ge(s_sdown, (EARLY + i + 1) * SJ)
                for b in range(2):
                    v = sum_a[EARLY + i][:, 2 * b:2 * b + 2, :].rearrange("p t n -> p (t n)")
                    if b == 0:
                        dve.wait_ge(s_add, EARLY + i + 1)
                    nc.vector.tensor_tensor(v, v, h_y[:, 2 * i + b], ALU.add).then_inc(s_done, 1)

        @block.tensor
        def _(pe):
            pe.wait_ge(s_q, 16 * 3)
            for k in range(KC):
                last = nc.tensor.matmul(ps_h[0][:, k * B:(k + 1) * B], w3_sb[:, k * P:(k + 1) * P], q_sb[:, :],
                                        start=True, stop=True)
            last.then_inc(s_qps, 1)
            pe.wait_ge(s_c1, 16 * 3)

            def transpose(dst, src):
                return nc.tensor.matmul(dst, src, ident_sb[:, :], is_transpose=True, start=True, stop=True)

            def logits(g):
                pe.wait_ge(s_hid, (g + 1) * KC)
                if g == 0:
                    pe.wait_ge(s_c2, 16 * 7)
                for i in range(TG):
                    c = (g * TG + i) * E
                    for k in range(KC):
                        last = nc.tensor.matmul(ps_logit[:, c:c + E], hid[g][:, k, i * P:(i + 1) * P], gate_sb[:, k],
                                                start=(k == 0), stop=(k == KC - 1))
                last.then_inc(s_gate, 1)

            def to_rows(g):
                for i in range(TG):
                    reuse(pe, s_row, g * TG + i - 1)
                    for k in range(KC):
                        last = transpose(ps_x[i % 2][:, k * P:(k + 1) * P], hid[g][:, k, i * P:(i + 1) * P])
                    last.then_inc(s_tr, 1)

            for g in range(NG):
                pe.wait_ge(s_z, g + 1)
                reuse(pe, s_hid, (g - 1) * KC)
                bank = ps_gu if g % 2 == 0 else ps_y
                for m in range(KC):
                    for k in range(KC):
                        last = nc.tensor.matmul(bank[m], w2c_sb[:, k, m * P:(m + 1) * P], x_g[g][:, k],
                                                start=(k == 0), stop=(k == KC - 1))
                last.then_inc(s_cond, 1)
                if g:
                    logits(g - 1)
                    to_rows(g - 1)
            logits(NG - 1)

            def shared_gu(n, halves=(0, 1)):
                g, j = n // SJ, n % SJ
                h = hid[g] if g < EARLY else hid_l[g - EARLY]
                if n == 0:
                    pe.wait_ge(s_sw, 32)
                if n == 1:
                    pe.wait_ge(s_row, NG * TG)
                if 0 in halves:
                    reuse(pe, s_smul, n - 1)
                for v in halves:
                    for k in range(KC):
                        last = nc.tensor.matmul(gu_x[:, 2 * (n % 2) + v], sw13[:, k, v, j * P:(j + 1) * P], h[:, k],
                                                start=(k == 0), stop=(k == KC - 1))
                if 1 in halves:
                    last.then_inc(s_sgu, 1)

            def shared_down(n):
                g, j = n // SJ, n % SJ
                pe.wait_ge(s_smul, n + 1)
                if g and g < EARLY:
                    pe.wait_ge(s_base, 2 * g)
                for i in range(TG):
                    bank = h_y[:, (2 if g < EARLY else 2 * (g - EARLY)) + i // 2]
                    last = nc.tensor.matmul(bank[:, (i % 2) * H:(i % 2 + 1) * H],
                                            shared_act(n)[:, i * P:(i + 1) * P], sw2[:, j],
                                            start=(j == 0 and i % 2 == 0), stop=(j == SJ - 1), skip_group_check=True)
                last.then_inc(s_sdown, 1)

            def place(t, b):
                pe.wait_ge(s_oh, t + 1)
                pe.wait_ge(s_hit, t + 1)
                for k in range(top_k):
                    last = nc.tensor.matmul(ps_idx[:, 0:NT], lo1[b][:, :, k], hi_tok[b][:, :, k],
                                            start=False, stop=False, skip_group_check=True)
                last.then_inc(s_idxmm, 1)

            def zero_pass(start):
                return nc.tensor.matmul(ps_idx[:, 0:NT], zeros_h[:, :], zeros_h[:, 0:NT],
                                        start=start, stop=not start, skip_group_check=True)

            shared_gu(0)
            to_rows(NG - 1)
            shared_gu(1)
            pe.wait_ge(s_mask, 1)
            pe.wait_ge(s_zero, 2)
            nc.tensor.matmul(ps_rank[:, 0:TE + E], tri_sb[:, :], mask[:, :, :], start=True, stop=False)
            for t in range(TT):
                n = TT - t
                last = nc.tensor.matmul(ps_rank[:, (t + 1) * E:TE + E], ones_sb[:, :],
                                        mask[:, t, :].unsqueeze(1).to_broadcast([P, n, E]),
                                        start=False, stop=(t == TT - 1))
            last.then_inc(s_rank, 1)
            shared_down(0)
            shared_gu(2)
            pe.wait_ge(s_tep, 1)
            nc.tensor.matmul(ps_rank[:, 0:NT], ones_sb[:, :], te_diag[:, 0:NT], start=True, stop=True).then_inc(s_teps, 1)
            shared_down(1)
            shared_gu(3)
            zero_pass(True)
            pair(place, 0)
            pair(place, 1)
            shared_down(2)
            pair(place, 2)
            shared_gu(4, halves=(0,))
            pair(place, 3)
            shared_gu(4, halves=(1,))
            pair(place, 4)
            shared_down(3)
            pair(place, 5)
            shared_gu(5, halves=(0,))
            pair(place, 6)
            pair(place, 7)
            zero_pass(False).then_inc(s_idxps, 1)
            shared_gu(5, halves=(1,))
            shared_down(4)
            shared_down(5)

            pe.wait_ge(s_te, 1)

            def experts(q):
                at = slice(q * RING, (q + 2) * RING) if isinstance(q, int) else bass.ds(q * RING, 2 * RING)
                return nc.values_load_multi_w_load_instructions(
                    te[0:1, at], engines=(mybir.EngineType.PE,), min_val=0, max_val=E - 1,
                    skip_runtime_bounds_check_because="te is a count of experts, cut to E - 1")[1]

            def step(s, r, q, tile_expert):
                if live(s):
                    pe.wait_ge(s_xgin[r], 16 * q + 16)
                    for k in range(KC):
                        last = transpose(ps_x[r % 2][:, k * P:(k + 1) * P], xg[:, r, k * P:(k + 1) * P])
                    last.then_inc(s_t1, 1)
                if live(s - 1):
                    b = (r - 1) % 2
                    e = tile_expert[r + 2]
                    if isinstance(s, int) and s == 1:
                        pe.wait_ge(s_wlo, len(PIECES))
                    pe.wait_ge(s_xlo, s + 1)
                    n = 0
                    for k in range(KC):
                        for a, w in ((x_hi, w13_hi), (x_hi, w13_lo), (x_lo, w13_hi)):
                            last = nc.tensor.matmul(ps_gu[b][:, 0:I2], a[:, b, k * P:(k + 1) * P], w[:, bass.ds(e, 1), k],
                                                    start=(n == 0), stop=(n == 3 * KC - 1))
                            n += 1
                    last.then_inc(s_gu, 1)
                if live(s - 2):
                    b = r % 2
                    pe.wait_ge(s_h, s + 1)
                    for k in range(KC):
                        last = transpose(ps_h[b][0:IC, k * P:(k + 1) * P], hid_e[:, b, k * IC:(k + 1) * IC])
                    last.then_inc(s_t2, 1)
                if live(s - 3):
                    b = (r - 3) % 2
                    e = tile_expert[r]
                    if isinstance(s, int) and s == 3:
                        pe.wait_ge(s_base, 2 * EARLY)
                    pe.wait_ge(s_alo, s + 1)
                    n = 0
                    for k in range(KC):
                        for a, w in ((a_hi, w2_hi), (a_hi, w2_lo), (a_lo, w2_hi)):
                            last = nc.tensor.matmul(ps_y[b][:, 0:H], a[:, b, k * P:(k + 1) * P], w[:, bass.ds(e, 1), k],
                                                    start=(n == 0), stop=(n == 3 * KC - 1))
                            n += 1
                    last.then_inc(s_yps, 1)

            pe.sem_inc(s_gu, 1)
            pe.sem_inc(s_t2, 2)
            pe.sem_inc(s_yps, 3)
            steps(pe, step, NT + 3, experts)

            pe.wait_ge(s_hl, 16 * (NG - EARLY))
            pe.wait_ge(s_yout, LAG + NT)
            for n in range(EARLY * SJ, NG * SJ):
                shared_gu(n)
                if n > EARLY * SJ:
                    shared_down(n - 1)
            shared_down(NG * SJ - 1)


_OUT = "out_0_dram"


def kernel(**inputs):
    import numpy as np
    import concourse.bacc as bacc
    import ml_dtypes
    from concourse.bass_utils import run_bass_kernel_spmd

    a = {k: np.asarray(v) for k, v in inputs.items()}
    x = a["x"]
    B, N, H = x.shape
    T, KC = B * N, H // P
    w13, w2, sw13, sw2 = (a["L0_ffn_" + n] for n in ("w13", "w2", "sw13", "sw2"))
    E, I2 = w13.shape[:2]
    I = I2 // 2
    IS = sw13.shape[0] // 2
    SJ = -(-IS // P)
    TT = T // P

    def chunks(m):
        return m.reshape(KC, P, -1).transpose(1, 0, 2)

    sg = np.zeros((KC, P, 2, SJ * P), np.float32)
    sg[..., :IS] = sw13.reshape(2, IS, KC, P).transpose(2, 3, 0, 1)
    sd = np.zeros((SJ * P, H), np.float32)
    sd[:IS] = sw2.T
    ar = np.arange
    ins = {
        "x_rows": x.reshape(T, H),
        "xT": chunks(x.reshape(T, H).T),
        "qT": a["cond_1024"].T,
        "w3": a["L0_cond_W3"],
        "b3": a["L0_cond_b3"].reshape(KC, P).T,
        "w2c": chunks(a["L0_cond_W2"]),
        "b2": a["L0_cond_b2"].reshape(KC, P).T,
        "gateT": chunks(a["L0_ffn_gate_w"].T),
        "w13T": w13.transpose(0, 2, 1).reshape(E, KC, P, I2),
        "w2T": w2.transpose(0, 2, 1).reshape(E, KC, I // KC, H),
        "sw13T": sg.transpose(1, 0, 2, 3),
        "sw2T": sd.reshape(SJ, P, H).transpose(1, 0, 2),
        "ident": np.eye(P, dtype=np.float32),
        "tri": np.triu(np.ones((P, P), np.float32), 1).astype(ml_dtypes.bfloat16),
        "ones": np.ones((P, P), ml_dtypes.bfloat16),
        "iota_e": np.tile(ar(E, dtype=np.float32), (P, 1)),
        "iota_k": np.tile(np.repeat(ar(P).astype(np.float16), 6).reshape(P, 6), (P, 1, 1)),
        "iota_p": ar(P, dtype=np.float32)[:, None],
        "token1": (ar(P)[:, None] + P * ar(TT)[None, :] + 1).astype(np.float32),
    }
    ins = {k: np.ascontiguousarray(v) for k, v in ins.items()}
    nc = bacc.Bacc("TRN2", target_bir_lowering=False, num_devices=1, dynamic_dma_scratch_size=8192)
    aps = {k: nc.dram_tensor(k, v.shape, mybir.dt.from_np(v.dtype), kind="ExternalInput").ap() for k, v in ins.items()}
    aps["out"] = nc.dram_tensor(_OUT, (T, H), F32, kind="ExternalOutput").ap()
    adaln_moe_ffn(nc, top_k=6, **aps)
    r = run_bass_kernel_spmd(nc, [ins], core_ids=[0])
    return r.results[0][_OUT].reshape(B, N, H)
```

```python
from contextlib import ExitStack

import concourse.bass as bass
from concourse import mybir
from concourse.alu_op_type import AluOpType as ALU

P = 128
TOP_K = 6
F32 = mybir.dt.float32
F32R = mybir.dt.float32r
BF16 = mybir.dt.bfloat16
F16 = mybir.dt.float16
I32 = mybir.dt.int32
U32 = mybir.dt.uint32
ACT = mybir.ActivationFunctionType
AX = mybir.AxisListType

RING = 4
LAG = 6
AHEAD = 3


def reuse(eng, sem, value):
    if not (isinstance(value, int) and value <= 0):
        eng.wait_ge(sem, value)


def adaln_moe_ffn(nc, x_rows, xT, qT, w3, b3, w2c, b2, gateT, w13T, w2T, sw13T, sw2T,
                  ident, tri, ones, iota_e, iota_k, iota_p, token1, out, top_k):
    T, H = x_rows.shape
    KC = H // P
    B = qT.shape[1]
    N = T // B
    E = gateT.shape[2]
    I2 = w13T.shape[3]
    I = I2 // 2
    IC = I // KC
    SJ = sw2T.shape[1]
    GT = 512
    NG = T // GT
    BG = GT // N
    TG = GT // P
    TT = T // P
    TK = TT * top_k
    NT = TK + E - 1
    ROUNDS = NT // RING
    EARLY = NG // 2
    W = H + 2 * top_k
    assert NT <= P

    hid_dram = nc.dram_tensor("hid_rows", (T, W), F32, kind="Internal").ap()
    sums = [nc.dram_tensor(f"sum{i}", (T + P, H), F32, kind="Internal").ap() for i in range(2)]
    late_dram = nc.dram_tensor("late_hid", (NG - EARLY, P, KC, GT), F32, kind="Internal").ap()

    with ExitStack() as ctx:
        def sb(name, shape, dt=F32):
            return ctx.enter_context(nc.sbuf_tensor(name, shape, dt))

        def sem(name):
            return ctx.enter_context(nc.semaphore(name))

        w13_hi = sb("w13_hi", [P, E, KC, I2], F32R)
        w13_lo = sb("w13_lo", [P, E, KC, I2], F32R)
        w2_hi = sb("w2_hi", [IC, E, KC, H], F32R)
        w2_lo = sb("w2_lo", [IC, E, KC, H], F32R)
        SW13, SW2 = KC * 2 * SJ * P, SJ * H
        def shared_weights(a):
            return (a[:, 0:SW13].rearrange("p (k v n) -> p k v n", k=KC, v=2),
                    a[:, SW13:SW13 + SW2].rearrange("p (j n) -> p j n", j=SJ))

        with nc.sbuf_tensor("x_gathered", [P, RING, W], F32) as xg:
            pass
        act_rest = sb("act_lo", [P, RING, W], F32R)
        x_hi = sb("x_hi", [P, 2, KC * P], F32R)
        x_lo = sb("x_lo", [P, 2, KC * P], F32R)
        sil_h = sb("silu_and_h", [P, 4, I])
        sil, hid_e = sil_h[:, 0:2], sil_h[:, 2:4]
        a_hi = sb("a_hi", [IC, 2, KC * P], F32R)
        a_lo = sb("a_lo", [IC, 2, KC * P], F32R)
        y_sb = sb("y_sb", [P, RING, H])
        gidx = sb("gather_index", [P, RING], U32)
        sidx = sb("scatter_index", [P, RING], U32)
        EL = 2
        SEL = TK * E
        R_END = GT * KC + SEL
        front_words = R_END + EARLY * KC * GT + TG * H + P * top_k + NT * top_k
        HL, SWN = (NG - EARLY) * KC * GT, SW13 + SW2
        assert 2 * HL + SWN <= front_words
        with nc.sbuf_tensor("arena", [P, front_words], F32) as arena, nc.sbuf_tensor("sw", [P, SWN], F32) as sw:
            pass
        late = sb("late_operands", [P, front_words], F32R)
        sw_rest = sb("shared_weights_lo", [P, SWN], F32R)
        sw13, sw2 = shared_weights(sw)
        at = [0]

        def carve(n, start=None):
            a = at[0] if start is None else start
            at[0] = a + n
            return arena[:, a:a + n]

        x_g = [carve(KC * GT).rearrange("p (k n) -> p k n", k=KC) for _ in range(2)]
        LATE_X = E - -(-(NG - 2) * KC * GT // (KC * I2))
        x_late = w13_hi[:, LATE_X:].rearrange("p e k n -> p (e k n)").bitcast(F32)
        x_g += [x_late[:, g * KC * GT:(g + 1) * KC * GT].rearrange("p (k n) -> p k n", k=KC) for g in range(NG - 2)]
        w2c_sb = carve(KC * H).rearrange("p (k n) -> p k n", k=KC)
        assert at[0] <= R_END
        act_f = carve(2 * GT, 0).rearrange("p (b n) -> p b n", b=2)
        sel = carve(SEL)
        early = [carve(KC * GT) for _ in range(EARLY)]
        rows = carve(TG * H)
        hid = [h.rearrange("p (k n) -> p k n", k=KC) for h in early]
        hid += [b[:, :, :].rearrange("p r n -> p (r n)")[:, 0:KC * GT].rearrange("p (k n) -> p k n", k=KC)
                for b in (xg, y_sb)]
        base = [h.rearrange("p (t n) -> p t n", t=TG) for h in early]
        rows4 = rows.rearrange("p (t n) -> p t n", t=TG)
        x_free = x_g[0].rearrange("p k n -> p (k n)")
        rows_g = [x_free.rearrange("p (t n) -> p t n", t=TG), rows4]
        OHL, OHH = P * top_k // 2, NT * top_k // 2
        iota_k_sb = carve(OHL).bitcast(F16).rearrange("p (n k) -> p n k", k=top_k)
        oh = [sel[:, 0:OHL + 2 * OHH], carve(OHL + 2 * OHH)]
        lo1 = [b[:, 0:OHL].bitcast(F16).rearrange("p (n k) -> p n k", k=top_k) for b in oh]
        hi1 = [b[:, OHL:OHL + OHH].bitcast(F16).rearrange("p (n k) -> p n k", k=top_k) for b in oh]
        hi_tok = [b[:, OHL + OHH:].bitcast(F16).rearrange("p (n k) -> p n k", k=top_k) for b in oh]
        SPLIT = 256
        hid_raw, hid_h, sw_h = arena[:, 0:HL], late[:, HL:2 * HL], late[:, 2 * HL:2 * HL + SWN]
        assert HL % SPLIT == 0 and SWN % SPLIT == 0
        splits = ((hid_raw, hid_h, late[:, 0:HL], HL // SPLIT), (sw[:, :], sw_h, sw_rest[:, :], SWN // SPLIT))

        def late_groups(a):
            return a.rearrange("p (g k n) -> p g k n", g=NG - EARLY, k=KC)

        hid_l = late_groups(hid_raw)
        hid_hi_lo = late_groups(hid_h), late_groups(late[:, 0:HL])
        sw_hi, sw_lo = shared_weights(sw_h), shared_weights(sw_rest)
        free = w13_hi[:, :, :, :].rearrange("p e k n -> p (e k n)").bitcast(F32)
        group_sums = [free[:, n * TG * H:(n + 1) * TG * H].rearrange("p (t n) -> p t n", t=TG) for n in range(2 * NG)]
        sum_a, sum_b = group_sums[:NG], group_sums[NG:]
        act_l, act_lo = (a[:, :, :].rearrange("p r n -> p (r n)")[:, 0:2 * GT].rearrange("p (b n) -> p b n", b=2)
                         for a in (xg, act_rest))
        act_hi = [x_hi[:, :, :].rearrange("p b n -> p (b n)"), late[:, 2 * HL + SWN:2 * HL + SWN + GT]]
        assert 2 * KC * P == GT and 2 * HL + SWN + GT <= front_words
        def r_words(a, n):
            return oh[1][:, a:a + n]
        TE = TT * E
        shifted = r_words(0, TE).rearrange("p (t e) -> p t e", e=E)
        expd = r_words(TE, TE).rearrange("p (t e) -> p t e", e=E)
        score = r_words(2 * TE, TE).rearrange("p (t e) -> p t e", e=E)
        slot_te = r_words(0, TE).rearrange("p (t e) -> p t e", e=E)
        top = r_words(3 * TE, TT * 8).rearrange("p (t k) -> p t k", k=8)
        topi = r_words(3 * TE + TT * 8, TT * 8).bitcast(U32).rearrange("p (t k) -> p t k", k=8)
        w_tok = sb("w_tok", [P, TT, 2, top_k])
        rsmall = sb("rsmall", [P, 3, TT])
        slot_i = r_words(TE, 3 * TK).bitcast(I32).rearrange("p (v n) -> p v n", v=3)
        slot_lo = sb("slot_lo", [P, TK], F16)
        slot_hi = sb("slot_hi", [P, TK], F16)
        mask = sb("mask", [P, TT + 1, E], BF16)
        esm = sb("esm", [P, 6, E])
        esi = sb("esi", [P, 2, E], I32)
        te_p = sb("te_p", [P, 1])
        te_diag = sb("te_diag", [P, P], BF16)
        te_all = sb("te_all", [P, NT])
        te = sb("te", [1, (ROUNDS + 3) * RING], I32)
        idx_f = r_words(TE, NT)
        idx_t = r_words(2 * TE, NT)
        g_all = sb("g_all", [P, NT], U32)
        s_all = sb("s_all", [P, NT], U32)
        w_pick = sb("w_pick", [P, RING, top_k])
        w_slot = sb("w_slot", [P, RING])
        past_end = sb("past_end", [P, 1])
        first_slot = sb("first_slot", [P, 1])
        ident_sb = sb("ident_sb", [P, P])
        tri_sb = sb("tri_sb", [P, P], BF16)
        ones_sb = sb("ones_sb", [P, P], BF16)
        iota_e_sb = sb("iota_e_sb", [P, E])
        iota_p_sb = sb("iota_p_sb", [P, 1])
        token1_sb = sb("token1_sb", [P, TT])
        q_sb = sb("q_sb", [P, B])
        w3_sb = sil_h[:, 0:2].rearrange("p a n -> p (a n)")[:, 0:H]
        vsum = sil_h[:, 2:4].rearrange("p a n -> p (a n)")[:, 0:2 * KC * BG].rearrange("p (b k n) -> p b k n", b=2, k=KC)
        qemb = sb("qemb", [P, KC, B])
        b3_sb = sb("b3_sb", [P, KC])
        b2_sb = sb("b2_sb", [P, KC])
        gate_sb = sb("gate_sb", [P, KC, E])
        zeros_h = sb("zeros_h", [P, P], F16)
        assert OHL + 2 * OHH + H <= SEL
        zero_row = sel[:, SEL - H:]

        gu_x = ctx.enter_context(nc.psum_tensor("gu_x", [P, 4, GT], F32))
        h_y = ctx.enter_context(nc.psum_tensor("h_y", [P, 4, GT], F32))
        ps_gu, ps_x = [gu_x[:, 0], gu_x[:, 1]], [gu_x[:, 2], gu_x[:, 3]]
        ps_h, ps_y = [h_y[:, 0], h_y[:, 1]], [h_y[:, 2], h_y[:, 3]]
        ps_rank, ps_logit, ps_idx = ps_h[0], ps_h[1], ps_h[1]

        s_q = sem("q_loaded")
        s_w2c = sem("w2c_loaded")
        s_c1 = sem("b2_gate_loaded")
        s_c2 = sem("constants_loaded")
        s_sw = sem("shared_weights_loaded")
        s_x0 = [sem(f"first_x_loaded{k}") for k in range(KC)]
        s_xin = [sem(f"x_group_loaded{g}") for g in range(NG)]
        s_raw = [sem(f"expert_weights_loaded{i}") for i in range(E // EL)]
        s_whi = sem("weights_hi")
        s_wlo = sem("weights_lo")
        s_qps = sem("qemb_in_psum")
        s_qemb = sem("qemb_ready")
        s_z = sem("z_ready")
        s_cond = sem("cond_in_psum")
        s_hid = sem("hid_ready")
        s_gate = sem("logits_in_psum")
        s_tr = sem("hid_transposed")
        s_row = sem("hid_rows_ready")
        s_rowst = [sem(f"hid_rows_stored{i}") for i in range(2)]
        s_late = sem("late_hid_stored")
        s_v = sem("vector_step")
        s_exp = sem("exp_ready")
        s_mask = sem("mask_ready")
        s_rank = sem("ranks_in_psum")
        s_tep = sem("tile_expert_column_ready")
        s_teps = sem("tile_expert_row_in_psum")
        s_te = sem("tile_expert_ready")
        s_hi1 = sem("tile_one_hots_ready")
        s_oh = sem("place_one_hots_ready")
        s_hit = sem("token_one_hots_ready")
        s_idxmm = sem("one_hots_used")
        s_idxps = sem("indices_in_psum")
        s_idx = sem("indices_ready")
        s_zero = sem("zeros_set")
        s_sgu = sem("shared_gate_up_in_psum")
        s_ssil = sem("shared_silu_ready")
        s_smul = sem("shared_act_ready")
        s_sdown = sem("shared_down_done")
        s_sum0 = sem("sums_initialised")
        s_wst = sem("weights_stored")
        s_w = sem("weights_ready")
        s_base = sem("base_ready")
        s_basest = sem("base_stored")
        s_gi = sem("gather_index_ready")
        s_xgin = [sem(f"x_gathered{i}") for i in range(RING)]
        s_t1 = sem("x_transposed")
        s_xhi = sem("x_hi_ready")
        s_xlo = sem("x_lo_ready")
        s_gu = sem("gate_up_in_psum")
        s_sil = sem("silu_ready")
        s_h = sem("h_ready")
        s_t2 = sem("h_transposed")
        s_ahi = sem("a_hi_ready")
        s_alo = sem("a_lo_ready")
        s_yps = sem("y_in_psum")
        s_yout = sem("y_ready")
        s_scat = [sem(f"y_scattered{i}") for i in range(RING)]
        s_carry = sem("carries_a_wait")
        s_hl = sem("late_hid_loaded")
        s_lhi = sem("late_operands_hi")
        s_llo = sem("late_operands_lo")
        s_acthi = sem("act_hi_ready")
        s_actlo = sem("act_lo_ready")
        s_suma = [sem(f"sum_loaded{g}") for g in range(NG)]
        s_add = sem("sums_added")
        s_done = sem("late_half_done")
        s_out = sem("out_stored")

        block = ctx.enter_context(nc.Block())

        def steps(eng, body, last, begin=None):
            rounds = range(-(-last // RING))
            for q in rounds[:1]:
                args = (begin(q),) if begin else ()
                for r in range(RING):
                    body(q * RING + r, r, q, *args)
            with eng.Fori(1, ROUNDS) as q:
                args = (begin(q),) if begin else ()
                for r in range(RING):
                    body(q * RING + r, r, q, *args)
            for q in rounds[ROUNDS:]:
                args = (begin(q),) if begin else ()
                for r in range(min(RING, last - q * RING)):
                    body(q * RING + r, r, q, *args)

        SPLIT_AT = 2

        def rounds_with_splits(eng, body, last, split):
            first = SPLIT_AT
            for src, hi, lo, n in splits:
                with eng.Fori(first, first + n) as q:
                    split(src, hi, lo, q - first, q - SPLIT_AT)
                    for r in range(RING):
                        body(q * RING + r, r, q)
                first += n
            with eng.Fori(first, last) as q:
                for r in range(RING):
                    body(q * RING + r, r, q)

        def live(t):
            return not isinstance(t, int) or 0 <= t < NT

        assert EARLY == 2 and SJ == 3 and TT == 16

        def pair(body, q):
            for b in range(2):
                body(2 * q + b, b)

        PIECES = [(e, part) for e in range(E) for part in range(2)]

        def split_piece(w13, w2, n):
            e, part = PIECES[n]
            return w13[:, e] if part == 0 else w2[:, e]

        @block.sync
        def _(sp):
            sp.dma_start(x_g[0][:, 0], xT[:, 0, 0:GT]).then_inc(s_x0[0], 16)
            sp.dma_start(w3_sb, w3).then_inc(s_q, 16)
            sp.dma_start(q_sb[:, :], qT).then_inc(s_q, 16)
            sp.dma_start(b3_sb[:, :], b3).then_inc(s_q, 16)
            sp.dma_start(w2c_sb, w2c).then_inc(s_w2c, 16)
            for k in range(1, KC):
                sp.dma_start(x_g[0][:, k], xT[:, k, 0:GT]).then_inc(s_x0[k], 16)
            sp.dma_start(b2_sb[:, :], b2).then_inc(s_c1, 16)
            sp.dma_start(x_g[1], xT[:, :, GT:2 * GT]).then_inc(s_xin[1], 16)
            sp.dma_start(gate_sb[:, :, :], gateT).then_inc(s_c1, 16)
            for g in range(2, NG):
                sp.dma_start(x_g[g], xT[:, :, g * GT:(g + 1) * GT]).then_inc(s_xin[g], 16)

            def load_weights(i):
                for lo, w in ((w13_lo, w13T), (w2_lo, w2T)):
                    sp.dma_start(lo[:, i * EL:(i + 1) * EL].bitcast(F32),
                                 w[i * EL:(i + 1) * EL].rearrange("e k p n -> p e k n")).then_inc(s_raw[i], 16)

            load_weights(0)
            for dst, src in ((ident_sb, ident), (tri_sb, tri), (ones_sb, ones), (iota_e_sb, iota_e),
                             (iota_p_sb, iota_p), (token1_sb, token1)):
                sp.dma_start(dst[:, :], src).then_inc(s_c2, 16)
            sp.dma_start(iota_k_sb, iota_k).then_inc(s_c2, 16)
            for i in range(1, E // EL):
                if i > 2:
                    sp.wait_ge(s_whi, 2 * EL * (i - 2))
                load_weights(i)
                if i == 3:
                    sp.dma_start(sw13, sw13T).then_inc(s_sw, 16)
                    sp.dma_start(sw2, sw2T).then_inc(s_sw, 16)

            def rows_of(dram, g):
                return dram[g * GT:(g + 1) * GT, :].rearrange("(t p) n -> p t n", p=P)

            sp.dma_start(sums[0][T:T + P, :], x_rows[0:P, :]).then_inc(s_sum0, 16)
            sp.dma_start(sums[1][T:T + P, :], x_rows[0:P, :]).then_inc(s_sum0, 16)
            for g in range(NG):
                sp.dma_start(sums[0][g * GT:(g + 1) * GT, :], x_rows[g * GT:(g + 1) * GT, :]).then_inc(s_sum0, 16)
            sp.wait_ge(s_w, 1)
            sp.dma_start(hid_dram[:, H:W].rearrange("(t p) k -> p t k", p=P),
                         w_tok[:, :, :, :].rearrange("p t a k -> p t (a k)")).then_inc(s_wst, 16)
            sp.wait_ge(s_zero, 3)
            for g in range(EARLY, NG):
                sp.dma_start(rows_of(sums[1], g), zero_row.unsqueeze(1).to_broadcast([P, TG, H])).then_inc(s_sum0, 16)
            for g in range(EARLY):
                sp.wait_ge(s_base, (g + 1) * 2)
                sp.dma_start(rows_of(sums[1], g), base[g]).then_inc(s_basest, 16)
            sp.wait_ge(s_basest, 16 * EARLY)
            sp.wait_ge(s_late, 16 * (NG - EARLY))
            sp.wait_ge(s_sum0, 16 * (2 + NG + NG - EARLY))
            sp.wait_ge(s_yout, LAG + 1)
            for g in range(NG - EARLY):
                sp.dma_start(hid_l[:, g], late_dram[g]).then_inc(s_hl, 16)
            for r in range(RING):
                sp.wait_ge(s_scat[r], 16 * len(range(r, NT, RING)))

            for g in range(NG):
                sp.dma_start(sum_a[g], rows_of(sums[0], g)).then_inc(s_suma[g], 16)
                sp.dma_start(sum_b[g], rows_of(sums[1], g)).then_inc(s_suma[g], 16)
            for g in range(EARLY):
                sp.wait_ge(s_add, g + 1)
                sp.dma_start(rows_of(out, g), sum_a[g]).then_inc(s_out, 16)
            for g in range(EARLY, NG):
                for b in range(2):
                    sp.wait_ge(s_done, 2 * (g - EARLY) + b + 1)
                    at_t = g * GT + b * GT // 2
                    sp.dma_start(out[at_t:at_t + GT // 2, :].rearrange("(t p) n -> p t n", p=P),
                                 sum_a[g][:, 2 * b:2 * b + 2, :]).then_inc(s_out, 16)
            sp.wait_ge(s_out, 16 * (EARLY + 2 * (NG - EARLY)))

        @block.gpsimd
        def _(pool):
            for n in range(len(PIECES)):
                pool.wait_ge(s_whi, n + 1)
                lo = split_piece(w13_lo, w2_lo, n)
                nc.gpsimd.tensor_sub(lo, lo.bitcast(F32), split_piece(w13_hi, w2_hi, n).bitcast(F32)).then_inc(s_wlo, 1)
            for b in range(2):
                pool.wait_ge(s_rowst[b], 16 * (NG // 2))
            pool.wait_ge(s_wst, 16)
            pool.wait_ge(s_late, 16 * (NG - EARLY))

            def step(s, r, q):
                if live(s):
                    pool.wait_ge(s_gi, s + 1)
                    pool.sem_inc(s_carry, 1)
                    nc.gpsimd.indirect_dma_start(
                        out=xg[:, r, :], out_offset=None, in_=hid_dram,
                        in_offset=bass.IndirectOffsetOnAxis(ap=gidx[:, r:r + 1], axis=0),
                        bounds_check=T - 1, oob_is_err=True).then_inc(s_xgin[r], 16)
                t, rt = s - LAG, (r - LAG) % RING
                if isinstance(t, int) and t == 0:
                    pool.wait_ge(s_sum0, 16 * (2 + NG + NG - EARLY))
                    pool.wait_ge(s_basest, 16 * EARLY)
                if live(t):
                    pool.wait_ge(s_yout, s + 1)
                    reuse(pool, s_scat[(rt - 2) % RING], 16 * (q + (r - LAG - 2) // RING + 1))
                    pool.sem_inc(s_carry, 1)
                    nc.gpsimd.indirect_dma_start(
                        out=sums[r % 2], out_offset=bass.IndirectOffsetOnAxis(ap=sidx[:, rt:rt + 1], axis=0),
                        in_=y_sb[:, rt, :], in_offset=None, compute_op=ALU.add,
                        bounds_check=T + P - 1, oob_is_err=True).then_inc(s_scat[rt], 16)

            for s in range(3 * RING):
                step(s, s % RING, s // RING)
            with pool.Fori(3, ROUNDS) as q:
                for r in range(RING):
                    step(q * RING + r, r, q)
            for s in range(ROUNDS * RING, NT + LAG):
                step(s, s % RING, s // RING)
            for r in range(RING):
                pool.wait_ge(s_scat[r], 16 * len(range(r, NT, RING)))
            for g in range(NG):
                pool.wait_ge(s_suma[g], 32)
                nc.gpsimd.tensor_tensor(sum_a[g], sum_a[g], sum_b[g], ALU.add).then_inc(s_add, 1)

        def unit_banks(n):
            b = (n + (n >= EARLY * SJ)) % 2
            return 2 * b, 2 * b + 1

        def shared_act(n):
            return (act_f if n < EARLY * SJ else act_l)[:, n % 2]

        SHIFTED = 2 * KC * NG + 2

        @block.scalar
        def _(act):
            split = [0]

            def split_hi(count):
                for _ in range(count):
                    n = split[0]
                    if n < len(PIECES):
                        act.wait_ge(s_raw[PIECES[n][0] // EL], 32)
                        nc.scalar.activation(split_piece(w13_hi, w2_hi, n), split_piece(w13_lo, w2_lo, n).bitcast(F32),
                                             ACT.Copy).then_inc(s_whi, 1)
                        split[0] += 1

            act.wait_ge(s_qps, 1)
            for k in range(KC):
                last = nc.scalar.activation(qemb[:, k], ps_h[0][:, k * B:(k + 1) * B], ACT.Relu, bias=b3_sb[:, k:k + 1])
            last.then_inc(s_qemb, 1)

            def to_rows(g):
                if g >= 2:
                    act.wait_ge(s_rowst[g % 2], 16 * (g // 2))
                for b in range(2):
                    act.wait_ge(s_tr, 2 * g + b + 1)
                    nc.scalar.activation(rows_g[g % 2][:, 2 * b:2 * b + 2].rearrange("p t n -> p (t n)"), ps_x[b],
                                         ACT.Copy).then_inc(s_row, 1)
                act.wait_ge(s_row, 2 * (g + 1))
                act.dma_start(hid_dram[g * GT:(g + 1) * GT, 0:H].rearrange("(t p) n -> p t n", p=P),
                              rows_g[g % 2]).then_inc(s_rowst[g % 2], 16)

            act.wait_ge(s_c1, 16 * 2)
            for g in range(NG):
                act.wait_ge(s_cond, g + 1)
                bank = ps_gu if g % 2 == 0 else ps_y
                for m in range(KC):
                    nc.scalar.activation(hid[g][:, m], bank[m], ACT.Relu, bias=b2_sb[:, m:m + 1]).then_inc(s_hid, 1)
                if g >= EARLY:
                    act.wait_ge(s_hid, (g + 1) * KC)
                    act.dma_start(late_dram[g - EARLY], hid[g]).then_inc(s_late, 16)
                if g:
                    to_rows(g - 1)
                split_hi(4 if g < NG - 1 else 2)
            assert 2 * LATE_X >= split[0]

            def shared_silu(n):
                act.wait_ge(s_sgu, n + 1)
                reuse(act, s_sdown, n - 1)
                nc.scalar.activation(shared_act(n), gu_x[:, unit_banks(n)[0]], ACT.Silu).then_inc(s_ssil, 1)

            def base_copy(g):
                act.wait_ge(s_sdown, (g + 1) * SJ)
                for b in range(2):
                    v = base[g][:, 2 * b:2 * b + 2, :].rearrange("p t n -> p (t n)")
                    nc.scalar.activation(v, ps_y[b], ACT.Copy).then_inc(s_base, 1)

            def scale_one_hots(t, b):
                tok = slice(t, t + 1)
                reuse(act, s_idxmm, t - 1)
                act.wait_ge(s_hi1, t + 1)
                nc.scalar.activation(hi_tok[b], hi1[b], ACT.Copy, scale=token1_sb[:, tok]).then_inc(s_hit, 1)

            act.wait_ge(s_v, SHIFTED)
            nc.scalar.activation(expd, shifted, ACT.Exp).then_inc(s_exp, 1)
            to_rows(NG - 1)
            split_hi(4)
            act.wait_ge(s_rowst[0], 16 * (NG // 2))
            shared_silu(0)
            split_hi(2)
            shared_silu(1)
            split_hi(6)
            shared_silu(2)
            split_hi(6)
            assert split[0] == len(PIECES)
            pair(scale_one_hots, 0)
            shared_silu(3)
            pair(scale_one_hots, 1)
            pair(scale_one_hots, 2)
            base_copy(0)
            pair(scale_one_hots, 3)
            shared_silu(4)
            for q in range(4, TT // 2):
                pair(scale_one_hots, q)
            shared_silu(5)

            def step(s, r, q):
                if isinstance(s, int) and s == 2:
                    base_copy(1)
                if live(s):
                    act.wait_ge(s_t1, s + 1)
                    nc.scalar.activation(x_hi[:, r % 2], ps_x[r % 2][:, 0:KC * P], ACT.Copy).then_inc(s_xhi, 1)
                if live(s - 1):
                    act.wait_ge(s_gu, s + 1)
                    nc.scalar.activation(sil[:, (r - 1) % 2], ps_gu[(r - 1) % 2][:, 0:I], ACT.Silu).then_inc(s_sil, 1)
                if live(s - 2):
                    act.wait_ge(s_t2, s + 1)
                    nc.scalar.activation(a_hi[:, r % 2], ps_h[r % 2][0:IC, 0:KC * P], ACT.Copy).then_inc(s_ahi, 1)

            act.sem_inc(s_sil, 1)
            act.sem_inc(s_ahi, 2)

            def split(src, hi, lo, c, done):
                nc.scalar.activation(hi[:, bass.ds(c * SPLIT, SPLIT)], src[:, bass.ds(c * SPLIT, SPLIT)], ACT.Copy)\
                  .then_inc(s_lhi, 1)

            for s in range(SPLIT_AT * RING):
                step(s, s % RING, s // RING)
            act.wait_ge(s_hl, 16 * (NG - EARLY))
            rounds_with_splits(act, step, ROUNDS, split)
            for s in range(ROUNDS * RING, NT + 3):
                step(s, s % RING, s // RING)
            for n in range(EARLY * SJ, NG * SJ):
                shared_silu(n)
                act.wait_ge(s_smul, n + 1)
                nc.scalar.activation(act_hi[n % 2], act_l[:, n % 2], ACT.Copy).then_inc(s_acthi, 1)

        @block.vector
        def _(dve):
            count = [0]

            def chain(ins):
                count[0] += 1
                ins.then_inc(s_v, 1)
                dve.wait_ge(s_v, count[0])

            nc.vector.memset(zeros_h[:, :], 0.0)
            nc.vector.memset(te[:, :], 0).then_inc(s_zero, 1)
            nc.vector.memset(mask[:, TT, :], 0.0).then_inc(s_zero, 1)
            for g in range(NG):
                for k in range(KC):
                    dve.wait_ge(s_x0[k] if g == 0 else s_xin[g], 16)
                    xk = x_g[g][:, k].rearrange("p (b n) -> p b n", n=N)
                    sum_k = vsum[:, g % 2, k, :]
                    chain(nc.vector.tensor_reduce(sum_k, xk, AX.X, ALU.add))
                    chain(nc.vector.scalar_tensor_tensor(xk, xk, float(N), sum_k.unsqueeze(2).to_broadcast([P, BG, N]),
                                                         ALU.mult, ALU.add))
                    if g == 0 and k == 0:
                        dve.wait_ge(s_qemb, 1)
                    q_k = qemb[:, k, g * BG:(g + 1) * BG].unsqueeze(2).to_broadcast([P, BG, N])
                    nc.vector.tensor_tensor(xk, xk, q_k, ALU.mult).then_inc(s_z, 1)

            def per_tile(a):
                return a.unsqueeze(2).to_broadcast([P, TT, E])

            def shared_mul(n):
                dve.wait_ge(s_ssil, n + 1)
                a = shared_act(n)
                nc.vector.tensor_tensor(a, a, gu_x[:, unit_banks(n)[1]], ALU.mult).then_inc(s_smul, 1)

            tiles, ends, begin, zero, le = (esm[:, n, :] for n in range(5))
            nc.vector.memset(zero, 0.0)
            rmax, esum, rec = (rsmall[:, n, :] for n in range(3))
            lg = ps_logit[:, 0:TE].rearrange("p (t e) -> p t e", e=E)
            dve.wait_ge(s_gate, NG)
            dve.wait_ge(s_c2, 16 * 7)
            nc.vector.tensor_scalar(first_slot[:, :], iota_p_sb[:, 0:1], float(P), None, ALU.mult)
            chain(nc.vector.tensor_reduce(rmax, lg, AX.X, ALU.max))
            chain(nc.vector.tensor_tensor(shifted, lg, per_tile(rmax), ALU.subtract))
            assert count[0] == SHIFTED
            dve.wait_ge(s_exp, 1)
            chain(nc.vector.tensor_reduce(esum, expd, AX.X, ALU.add))
            chain(nc.vector.reciprocal(rec, esum))
            chain(nc.vector.tensor_tensor(score, expd, per_tile(rec), ALU.mult))
            for t in range(TT):
                last = nc.vector.max(top[:, t], score[:, t])
            chain(last)
            for t in range(TT):
                last = nc.vector.max_index(topi[:, t], top[:, t], score[:, t])
            chain(last)
            sel_v = sel.rearrange("p (j e) -> p j e", e=E)
            sel4 = sel.rearrange("p (t k e) -> p t k e", k=top_k, e=E)
            chain(nc.vector.tensor_tensor(sel4, topi[:, :, 0:top_k].unsqueeze(3).to_broadcast([P, TT, top_k, E]),
                                          iota_e_sb[:, :].unsqueeze(1).unsqueeze(1).to_broadcast([P, TT, top_k, E]),
                                          ALU.is_equal))
            with nc.allow_low_precision("a mask of zeros and ones"):
                nc.vector.tensor_reduce(mask[:, 0:TT, :], sel.rearrange("p (t k e) -> p t e k", k=top_k, e=E),
                                        AX.X, ALU.add).then_inc(s_mask, 1)
            chain(nc.vector.tensor_reduce(esum, top[:, :, 0:top_k], AX.X, ALU.add))
            chain(nc.vector.tensor_scalar_add(rmax, esum, 1e-20))
            chain(nc.vector.reciprocal(rec, rmax))
            chain(nc.vector.tensor_tensor(w_tok[:, :, 0], top[:, :, 0:top_k],
                                          rec.unsqueeze(2).to_broadcast([P, TT, top_k]), ALU.mult))
            nc.vector.tensor_copy(w_tok[:, :, 1], topi[:, :, 0:top_k]).then_inc(s_w, 1)
            shared_mul(0)
            shared_mul(1)
            dve.wait_ge(s_rank, 1)
            chain(nc.vector.tensor_scalar(esi[:, 0, :], ps_rank[:, TE:TE + E], float(P - 1), None, ALU.add))
            chain(nc.vector.tensor_scalar(esi[:, 1, :], esi[:, 0, :], -P, None, ALU.bitwise_and))
            chain(nc.vector.tensor_copy(tiles, esi[:, 1, :]))
            chain(nc.vector.tensor_tensor_scan(ends, tiles, zero, 0.0, ALU.add, ALU.add))
            chain(nc.vector.tensor_tensor(begin, ends, tiles, ALU.subtract))
            chain(nc.vector.tensor_tensor(slot_te, ps_rank[:, 0:TE].rearrange("p (t e) -> p t e", e=E),
                                          begin.unsqueeze(1).to_broadcast([P, TT, E]), ALU.add))
            chain(nc.vector.tensor_tensor(sel4, sel4, slot_te.unsqueeze(2).to_broadcast([P, TT, top_k, E]), ALU.mult))
            with nc.allow_low_precision("whole numbers below 2^24, one of them not zero"):
                chain(nc.vector.tensor_reduce(slot_i[:, 0, :], sel_v, AX.X, ALU.add))
            nc.vector.tensor_scalar(slot_i[:, 2, :], slot_i[:, 0, :], 7, None, ALU.arith_shift_right)
            chain(nc.vector.tensor_scalar(slot_i[:, 1, :], slot_i[:, 0, :], P - 1, None, ALU.bitwise_and))
            nc.vector.tensor_copy(slot_hi[:, :], slot_i[:, 2, :])
            chain(nc.vector.tensor_copy(slot_lo[:, :], slot_i[:, 1, :]))

            def one_hots(t, b):
                of_tile = slice(t * top_k, (t + 1) * top_k)
                for dst, of_slot, n, ready, read in ((hi1[b], slot_hi, NT, s_hi1, s_hit), (lo1[b], slot_lo, P, s_oh, s_idxmm)):
                    reuse(dve, read, t - 1)
                    nc.vector.tensor_tensor(dst, iota_k_sb[:, 0:n],
                                            of_slot[:, of_tile].unsqueeze(1).to_broadcast([P, n, top_k]),
                                            ALU.is_equal).then_inc(ready, 1)

            shared_mul(2)
            pair(one_hots, 0)
            chain(nc.vector.tensor_scalar(le, ends, first_slot[:, 0:1], None, ALU.is_le))
            chain(nc.vector.tensor_reduce(te_p[:, :], le, AX.X, ALU.add))
            chain(nc.vector.tensor_scalar_min(te_p[:, :], te_p[:, :], float(E - 1)))
            nc.vector.tensor_scalar(te_diag[:, :], ident_sb[:, :], te_p[:, 0:1], None, ALU.mult).then_inc(s_tep, 1)
            pair(one_hots, 1)
            shared_mul(3)
            pair(one_hots, 2)
            pair(one_hots, 3)
            dve.wait_ge(s_teps, 1)
            nc.vector.tensor_copy(te[:, 3:3 + NT], ps_rank[0:1, 0:NT]).then_inc(s_te, 1)
            nc.vector.tensor_copy(te_all[:, :], ps_rank[:, 0:NT])
            nc.vector.memset(zero_row, 0.0).then_inc(s_zero, 1)
            pair(one_hots, 4)
            shared_mul(4)
            for q in range(5, TT // 2):
                pair(one_hots, q)

            def gather_index(s, r):
                col = slice(s, s + 1) if isinstance(s, int) else bass.ds(s, 1)
                nc.vector.tensor_copy(gidx[:, r:r + 1], g_all[:, col]).then_inc(s_gi, 1)

            dve.wait_ge(s_idxps, 1)
            chain(nc.vector.tensor_copy(idx_f, ps_idx[:, 0:NT]))
            chain(nc.vector.tensor_scalar(g_all[:, :], idx_f, -1.0, 0.0, ALU.add, ALU.max))
            dve.wait_ge(s_late, 16 * (NG - EARLY))
            for s in range(AHEAD + 1):
                gather_index(s, s)
            chain(nc.vector.tensor_scalar(past_end[:, :], iota_p_sb[:, 0:1], float(T + 1), None, ALU.add))
            chain(nc.vector.tensor_scalar(idx_t, idx_f, 0.0, past_end[:, 0:1], ALU.is_equal, ALU.mult))
            chain(nc.vector.scalar_tensor_tensor(s_all[:, :], idx_f, -1.0, idx_t, ALU.add, ALU.add))

            shared_mul(5)

            def step(s, r, q):
                if live(s):
                    dve.wait_ge(s_xhi, s + 1)
                    col = slice(s, s + 1) if isinstance(s, int) else bass.ds(s, 1)
                    nc.vector.scalar_tensor_tensor(w_pick[:, r], xg[:, r, H + top_k:W], te_all[:, col],
                                                   xg[:, r, H:H + top_k],
                                                   ALU.is_equal, ALU.mult, accum_out=w_slot[:, r:r + 1])
                    nc.vector.tensor_tensor(x_lo[:, r % 2], ps_x[r % 2][:, 0:KC * P], x_hi[:, r % 2].bitcast(F32),
                                            ALU.subtract).then_inc(s_xlo, 1)
                if not isinstance(s, int) or 0 < s < NT - AHEAD:
                    gather_index(s + AHEAD, (r + AHEAD) % RING)
                if live(s - 1):
                    b = (r - 1) % 2
                    dve.wait_ge(s_sil, s + 1)
                    w = w_slot[:, (r - 1) % RING:(r - 1) % RING + 1]
                    nc.vector.scalar_tensor_tensor(hid_e[:, b], sil[:, b], w, ps_gu[b][:, I:I2],
                                                   ALU.mult, ALU.mult).then_inc(s_h, 1)
                if live(s - 2):
                    dve.wait_ge(s_ahi, s + 1)
                    nc.vector.tensor_tensor(a_lo[:, r % 2], ps_h[r % 2][0:IC, 0:KC * P], a_hi[:, r % 2].bitcast(F32),
                                            ALU.subtract).then_inc(s_alo, 1)
                if live(s - 3):
                    rt = (r - 3) % RING
                    reuse(dve, s_scat[rt], 16 * (q + (r - 3) // RING))
                    t = s - 3
                    col = slice(t, t + 1) if isinstance(t, int) else bass.ds(t, 1)
                    nc.vector.tensor_copy(sidx[:, rt:rt + 1], s_all[:, col])
                    dve.wait_ge(s_yps, s + 1)
                    nc.vector.tensor_copy(y_sb[:, rt], ps_y[rt % 2][:, 0:H]).then_inc(s_yout, 1)

            dve.sem_inc(s_xlo, 1)
            dve.sem_inc(s_h, 2)
            dve.sem_inc(s_alo, 3)
            dve.sem_inc(s_yout, LAG)
            for s in range(2 * RING):
                step(s, s % RING, s // RING)

            def split(src, hi, lo, c, done):
                at_c = bass.ds(c * SPLIT, SPLIT)
                dve.wait_ge(s_lhi, done + 1)
                nc.vector.tensor_tensor(lo[:, at_c], src[:, at_c], hi[:, at_c].bitcast(F32),
                                        ALU.subtract).then_inc(s_llo, 1)

            rounds_with_splits(dve, step, ROUNDS - 1, split)
            for s in range((ROUNDS - 1) * RING, NT + 3):
                step(s, s % RING, s // RING)

            def add_shared(i):
                dve.wait_ge(s_sdown, (EARLY + i + 1) * SJ)
                dve.wait_ge(s_add, EARLY + i + 1)
                for b in range(2):
                    v = sum_a[EARLY + i][:, 2 * b:2 * b + 2, :].rearrange("p t n -> p (t n)")
                    nc.vector.tensor_tensor(v, v, h_y[:, 2 * i + b], ALU.add).then_inc(s_done, 1)

            for n in range(EARLY * SJ, NG * SJ):
                shared_mul(n)
                dve.wait_ge(s_acthi, n - EARLY * SJ + 1)
                nc.vector.tensor_tensor(act_lo[:, n % 2], act_l[:, n % 2], act_hi[n % 2].bitcast(F32),
                                        ALU.subtract).then_inc(s_actlo, 1)
            for i in range(NG - EARLY):
                add_shared(i)

        @block.tensor
        def _(pe):
            pe.wait_ge(s_q, 16 * 3)
            for k in range(KC):
                last = nc.tensor.matmul(ps_h[0][:, k * B:(k + 1) * B], w3_sb[:, k * P:(k + 1) * P], q_sb[:, :],
                                        start=True, stop=True)
            last.then_inc(s_qps, 1)
            pe.wait_ge(s_w2c, 16)

            def transpose(dst, src):
                return nc.tensor.matmul(dst, src, ident_sb[:, :], is_transpose=True, start=True, stop=True)

            def logits(g):
                pe.wait_ge(s_hid, (g + 1) * KC)
                if g == 0:
                    pe.wait_ge(s_c1, 16 * 2)
                    pe.wait_ge(s_c2, 16 * 7)
                for i in range(TG):
                    c = (g * TG + i) * E
                    for k in range(KC):
                        last = nc.tensor.matmul(ps_logit[:, c:c + E], hid[g][:, k, i * P:(i + 1) * P], gate_sb[:, k],
                                                start=(k == 0), stop=(k == KC - 1))
                last.then_inc(s_gate, 1)

            def to_rows(g):
                for b in range(2):
                    reuse(pe, s_row, 2 * (g - 1) + b + 1)
                    for i in range(2 * b, 2 * b + 2):
                        for k in range(KC):
                            at_i = (i % 2) * H + k * P
                            last = transpose(ps_x[b][:, at_i:at_i + P], hid[g][:, k, i * P:(i + 1) * P])
                    last.then_inc(s_tr, 1)

            for g in range(NG):
                reuse(pe, s_hid, (g - 1) * KC)
                bank = ps_gu if g % 2 == 0 else ps_y
                for k in range(KC):
                    pe.wait_ge(s_z, g * KC + k + 1)
                    for m in range(KC):
                        last = nc.tensor.matmul(bank[m], w2c_sb[:, k, m * P:(m + 1) * P], x_g[g][:, k],
                                                start=(k == 0), stop=(k == KC - 1))
                last.then_inc(s_cond, 1)
                if g:
                    logits(g - 1)
                    to_rows(g - 1)
            logits(NG - 1)

            def shared_gu(n, halves=(0, 1)):
                g, j = n // SJ, n % SJ
                h = hid[g]
                if n == 0:
                    pe.wait_ge(s_sw, 32)
                if n == 1:
                    pe.wait_ge(s_row, 2 * NG)
                if 0 in halves:
                    reuse(pe, s_smul, n - 1)
                for v in halves:
                    for k in range(KC):
                        last = nc.tensor.matmul(gu_x[:, unit_banks(n)[v]], sw13[:, k, v, j * P:(j + 1) * P], h[:, k],
                                                start=(k == 0), stop=(k == KC - 1))
                if 1 in halves:
                    last.then_inc(s_sgu, 1)

            def shared_down(n):
                g, j = n // SJ, n % SJ
                pe.wait_ge(s_smul, n + 1)
                if g and g < EARLY:
                    pe.wait_ge(s_base, 2 * g)
                for i in range(TG):
                    bank = h_y[:, 2 + i // 2]
                    last = nc.tensor.matmul(bank[:, (i % 2) * H:(i % 2 + 1) * H],
                                            shared_act(n)[:, i * P:(i + 1) * P], sw2[:, j],
                                            start=(j == 0 and i % 2 == 0), stop=(j == SJ - 1), skip_group_check=True)
                last.then_inc(s_sdown, 1)

            def place(t, b):
                pe.wait_ge(s_oh, t + 1)
                pe.wait_ge(s_hit, t + 1)
                for k in range(top_k):
                    last = nc.tensor.matmul(ps_idx[:, 0:NT], lo1[b][:, :, k], hi_tok[b][:, :, k],
                                            start=False, stop=False, skip_group_check=True)
                last.then_inc(s_idxmm, 1)

            def zero_pass(start):
                return nc.tensor.matmul(ps_idx[:, 0:NT], zeros_h[:, :], zeros_h[:, 0:NT],
                                        start=start, stop=not start, skip_group_check=True)

            shared_gu(0)
            to_rows(NG - 1)
            shared_gu(1)
            pe.wait_ge(s_mask, 1)
            pe.wait_ge(s_zero, 2)
            nc.tensor.matmul(ps_rank[:, 0:TE + E], tri_sb[:, :], mask[:, :, :], start=True, stop=False)
            for t in range(TT):
                n = TT - t
                last = nc.tensor.matmul(ps_rank[:, (t + 1) * E:TE + E], ones_sb[:, :],
                                        mask[:, t, :].unsqueeze(1).to_broadcast([P, n, E]),
                                        start=False, stop=(t == TT - 1))
            last.then_inc(s_rank, 1)
            shared_down(0)
            shared_gu(2)
            shared_down(1)
            shared_gu(3)
            zero_pass(True)
            pair(place, 0)
            shared_down(2)
            pair(place, 1)
            pe.wait_ge(s_tep, 1)
            nc.tensor.matmul(ps_rank[:, 0:NT], ones_sb[:, :], te_diag[:, 0:NT], start=True, stop=True).then_inc(s_teps, 1)
            shared_gu(4, halves=(0,))
            pair(place, 2)
            shared_gu(4, halves=(1,))
            pair(place, 3)
            shared_down(3)
            pair(place, 4)
            shared_gu(5, halves=(0,))
            pair(place, 5)
            shared_gu(5, halves=(1,))
            pair(place, 6)
            pair(place, 7)
            zero_pass(False).then_inc(s_idxps, 1)
            shared_down(4)
            shared_down(5)

            pe.wait_ge(s_te, 1)

            def experts(q):
                at = slice(q * RING, (q + 2) * RING) if isinstance(q, int) else bass.ds(q * RING, 2 * RING)
                return nc.values_load_multi_w_load_instructions(
                    te[0:1, at], engines=(mybir.EngineType.PE,), min_val=0, max_val=E - 1,
                    skip_runtime_bounds_check_because="te is a count of experts, cut to E - 1")[1]

            def late_gu(n):
                i, j = n // SJ - EARLY, n % SJ
                reuse(pe, s_smul, n - 1)
                for v in range(2):
                    m = 0
                    for k in range(KC):
                        for (w, _), h in ((sw_hi, hid_hi_lo[0]), (sw_lo, hid_hi_lo[0]), (sw_hi, hid_hi_lo[1])):
                            last = nc.tensor.matmul(gu_x[:, unit_banks(n)[v]], w[:, k, v, j * P:(j + 1) * P], h[:, i, k],
                                                    start=(m == 0), stop=(m == 3 * KC - 1))
                            m += 1
                last.then_inc(s_sgu, 1)

            def step(s, r, q, tile_expert):
                if isinstance(s, int) and s == NT + 2:
                    pe.wait_ge(s_llo, sum(n for _, _, _, n in splits))
                    late_gu(EARLY * SJ)
                if live(s):
                    pe.wait_ge(s_xgin[r], 16 * q + 16)
                    for k in range(KC):
                        last = transpose(ps_x[r % 2][:, k * P:(k + 1) * P], xg[:, r, k * P:(k + 1) * P])
                    last.then_inc(s_t1, 1)
                if live(s - 1):
                    b = (r - 1) % 2
                    e = tile_expert[r + 2]
                    if isinstance(s, int) and s == 1:
                        pe.wait_ge(s_wlo, len(PIECES))
                    pe.wait_ge(s_xlo, s + 1)
                    n = 0
                    for k in range(KC):
                        for a, w in ((x_hi, w13_hi), (x_hi, w13_lo), (x_lo, w13_hi)):
                            last = nc.tensor.matmul(ps_gu[b][:, 0:I2], a[:, b, k * P:(k + 1) * P], w[:, bass.ds(e, 1), k],
                                                    start=(n == 0), stop=(n == 3 * KC - 1))
                            n += 1
                    last.then_inc(s_gu, 1)
                if live(s - 2):
                    b = r % 2
                    pe.wait_ge(s_h, s + 1)
                    for k in range(KC):
                        last = transpose(ps_h[b][0:IC, k * P:(k + 1) * P], hid_e[:, b, k * IC:(k + 1) * IC])
                    last.then_inc(s_t2, 1)
                if live(s - 3):
                    b = (r - 3) % 2
                    e = tile_expert[r]
                    if isinstance(s, int) and s == 3:
                        pe.wait_ge(s_base, 2 * EARLY)
                    pe.wait_ge(s_alo, s + 1)
                    n = 0
                    for k in range(KC):
                        for a, w in ((a_hi, w2_hi), (a_hi, w2_lo), (a_lo, w2_hi)):
                            last = nc.tensor.matmul(ps_y[b][:, 0:H], a[:, b, k * P:(k + 1) * P], w[:, bass.ds(e, 1), k],
                                                    start=(n == 0), stop=(n == 3 * KC - 1))
                            n += 1
                    last.then_inc(s_yps, 1)

            pe.sem_inc(s_gu, 1)
            pe.sem_inc(s_t2, 2)
            pe.sem_inc(s_yps, 3)
            steps(pe, step, NT + 3, experts)

            def late_down(n):
                i, j = n // SJ - EARLY, n % SJ
                pe.wait_ge(s_actlo, n - EARLY * SJ + 1)
                for t in range(TG):
                    bank = h_y[:, 2 * i + t // 2]
                    for m, (a, (_, w)) in enumerate(((act_hi[n % 2], sw_hi), (act_hi[n % 2], sw_lo), (act_lo[:, n % 2], sw_hi))):
                        last = nc.tensor.matmul(bank[:, (t % 2) * H:(t % 2 + 1) * H],
                                                a[:, t * P:(t + 1) * P], w[:, j],
                                                start=(j == 0 and t % 2 == 0 and m == 0), stop=(j == SJ - 1 and m == 2),
                                                skip_group_check=True)
                last.then_inc(s_sdown, 1)

            late_gu(EARLY * SJ + 1)
            pe.wait_ge(s_yout, LAG + NT)
            for n in range(EARLY * SJ + 2, NG * SJ):
                late_gu(n)
                late_down(n - 2)
            for n in range(NG * SJ - 2, NG * SJ):
                late_down(n)


_OUT = "out_0_dram"


def kernel(**inputs):
    import numpy as np
    import concourse.bacc as bacc
    import ml_dtypes
    from concourse.bass_utils import run_bass_kernel_spmd

    a = {k: np.asarray(v) for k, v in inputs.items()}
    x = a["x"]
    B, N, H = x.shape
    T, KC = B * N, H // P
    w13, w2, sw13, sw2 = (a["L0_ffn_" + n] for n in ("w13", "w2", "sw13", "sw2"))
    E, I2 = w13.shape[:2]
    I = I2 // 2
    IS = sw13.shape[0] // 2
    SJ = -(-IS // P)
    TT = T // P

    def chunks(m):
        return m.reshape(KC, P, -1).transpose(1, 0, 2)

    sg = np.zeros((KC, P, 2, SJ * P), np.float32)
    sg[..., :IS] = sw13.reshape(2, IS, KC, P).transpose(2, 3, 0, 1)
    sd = np.zeros((SJ * P, H), np.float32)
    sd[:IS] = sw2.T
    ar = np.arange
    ins = {
        "x_rows": x.reshape(T, H),
        "xT": chunks(x.reshape(T, H).T),
        "qT": a["cond_1024"].T,
        "w3": a["L0_cond_W3"],
        "b3": a["L0_cond_b3"].reshape(KC, P).T,
        "w2c": chunks(a["L0_cond_W2"]),
        "b2": a["L0_cond_b2"].reshape(KC, P).T,
        "gateT": chunks(a["L0_ffn_gate_w"].T),
        "w13T": w13.transpose(0, 2, 1).reshape(E, KC, P, I2),
        "w2T": w2.transpose(0, 2, 1).reshape(E, KC, I // KC, H),
        "sw13T": sg.transpose(1, 0, 2, 3),
        "sw2T": sd.reshape(SJ, P, H).transpose(1, 0, 2),
        "ident": np.eye(P, dtype=np.float32),
        "tri": np.triu(np.ones((P, P), np.float32), 1).astype(ml_dtypes.bfloat16),
        "ones": np.ones((P, P), ml_dtypes.bfloat16),
        "iota_e": np.tile(ar(E, dtype=np.float32), (P, 1)),
        "iota_k": np.tile(np.repeat(ar(P).astype(np.float16), TOP_K).reshape(P, TOP_K), (P, 1, 1)),
        "iota_p": ar(P, dtype=np.float32)[:, None],
        "token1": (ar(P)[:, None] + P * ar(TT)[None, :] + 1).astype(np.float32),
    }
    ins = {k: np.ascontiguousarray(v) for k, v in ins.items()}
    nc = bacc.Bacc("TRN2", target_bir_lowering=False, num_devices=1, dynamic_dma_scratch_size=8192)
    aps = {k: nc.dram_tensor(k, v.shape, mybir.dt.from_np(v.dtype), kind="ExternalInput").ap() for k, v in ins.items()}
    aps["out"] = nc.dram_tensor(_OUT, (T, H), F32, kind="ExternalOutput").ap()
    adaln_moe_ffn(nc, top_k=TOP_K, **aps)
    r = run_bass_kernel_spmd(nc, [ins], core_ids=[0])
    return r.results[0][_OUT].reshape(B, N, H)
```
